# Optimizing a Trainium2 kernel written in Bass

```python
import numpy as np
import jax
import jax.numpy as jnp

def _softmax(x, axis=-1):
    return jax.nn.softmax(x, axis=axis)

def _gelu(x):
    return jax.nn.gelu(x, approximate=True)

def _silu(x):
    return jax.nn.silu(x)

def _sigmoid(x):
    return jax.nn.sigmoid(x)

def _layernorm(x, axis=-1, eps=1e-05):
    m = jnp.mean(x, axis=axis, keepdims=True)
    v = jnp.var(x, axis=axis, keepdims=True)
    return (x - m) / jnp.sqrt(v + eps)

def _scatter_add(tgt, idx, src, axis=0):
    return tgt.at[idx].add(src)

def _segment_sum(src, seg, n):
    return jax.ops.segment_sum(src, seg, n)
kernel_name = 'mk_sandwich_d1_jaxref_r8_aa7bfe'

def setup_inputs(seed: int=0):
    np.random.seed(seed)
    _w = jnp.asarray

    def _L0_attn_setup():
        import jax, jax.numpy as jnp
        import numpy as np
        BASE_FREQUENCY = 10000.0
        LRP = 17
        MIN_L = 1.0 - LRP / 100.0
        SDT_L = (BASE_FREQUENCY - MIN_L * BASE_FREQUENCY) * 2.0
        ARM_ATTENTION = 2.0
        HEADS_DIM = 64

        def _nrope(xs, base, angle_range):
            N, T, d = xs.shape
            half = d // 2
            inv_freq = base ** (-jnp.arange(half, dtype=jnp.float32) / half)
            pos = jnp.arange(T, dtype=jnp.float32)
            scale = angle_range / jnp.maximum(T - 1, 1)
            ang = pos[:, None] * inv_freq[None, :] * scale
            cos, sin = (jnp.cos(ang), jnp.sin(ang))
            x1, x2 = (xs[..., :half], xs[..., half:])
            return jnp.concatenate([x1 * cos - x2 * sin, x1 * sin + x2 * cos], axis=-1)
        key = jax.random.key(seed)
        ks = jax.random.split(key, 9)
        B, T, E = (4, 128, 128)
        x = jax.random.normal(ks[0], (B, T, E), dtype=jnp.float32)

        def w(k):
            return jax.random.normal(k, (E, E), dtype=jnp.float32) * 0.02
        z = jnp.zeros((E,), dtype=jnp.float32)
        return {'x': x, 'Wq': w(ks[1]), 'bq': z, 'Wk': w(ks[2]), 'bk': z, 'Wv': w(ks[3]), 'bv': z, 'Wo': w(ks[4]), 'bo': z, 'nrope_freq': jnp.zeros((1,), dtype=jnp.float32)}
    _L0_attn_in = _L0_attn_setup()

    def _L0_ffn_setup():
        import jax, jax.numpy as jnp
        import numpy as np
        B, C, D, O = (4, 512, 128, 128)
        PROJ = 32
        RANKS = [1, 2, 4, 8]
        E = len(RANKS)
        CLAMP_MAX = float(np.log(1.0 / 0.01))

        def _l2norm(v, axis):
            return v / jnp.maximum(jnp.linalg.norm(v, axis=axis, keepdims=True), 1e-12)
        key = jax.random.key(seed)
        ks = jax.random.split(key, 16)
        inp = {'x': jax.random.normal(ks[0], (B, C, D), dtype=jnp.float32), 'W': jax.random.normal(ks[1], (O, D), dtype=jnp.float32) / np.sqrt(D), 'Wp': jax.random.normal(ks[2], (PROJ, D), dtype=jnp.float32) / np.sqrt(D), 'bp': jnp.zeros((PROJ,), dtype=jnp.float32), 'sim': jax.random.normal(ks[3], (PROJ, E), dtype=jnp.float32) * 0.01, 'temp': jnp.full((1,), np.log(1.0 / 0.5), dtype=jnp.float32)}
        for i, r in enumerate(RANKS):
            inp[f'Wd{i}'] = jax.random.normal(ks[4 + 2 * i], (r, D), dtype=jnp.float32) / r
            inp[f'Wu{i}'] = jax.random.normal(ks[5 + 2 * i], (O, r), dtype=jnp.float32) * 0.01
        return inp
    _L0_ffn_in = _L0_ffn_setup()
    _d = {'L0_attn_x': _L0_attn_in['x'], 'L0_attn_Wq': _L0_attn_in['Wq'], 'L0_attn_bq': _L0_attn_in['bq'], 'L0_attn_Wk': _L0_attn_in['Wk'], 'L0_attn_bk': _L0_attn_in['bk'], 'L0_attn_Wv': _L0_attn_in['Wv'], 'L0_attn_bv': _L0_attn_in['bv'], 'L0_attn_Wo': _L0_attn_in['Wo'], 'L0_attn_bo': _L0_attn_in['bo'], 'L0_attn_nrope_freq': _L0_attn_in['nrope_freq'], 'L0_ffn_W': _L0_ffn_in['W'], 'L0_ffn_Wp': _L0_ffn_in['Wp'], 'L0_ffn_bp': _L0_ffn_in['bp'], 'L0_ffn_sim': _L0_ffn_in['sim'], 'L0_ffn_temp': _L0_ffn_in['temp'], 'L0_ffn_Wd0': _L0_ffn_in['Wd0'], 'L0_ffn_Wu0': _L0_ffn_in['Wu0'], 'L0_ffn_Wd1': _L0_ffn_in['Wd1'], 'L0_ffn_Wu1': _L0_ffn_in['Wu1'], 'L0_ffn_Wd2': _L0_ffn_in['Wd2'], 'L0_ffn_Wu2': _L0_ffn_in['Wu2'], 'L0_ffn_Wd3': _L0_ffn_in['Wd3'], 'L0_ffn_Wu3': _L0_ffn_in['Wu3']}
    _x0 = _d['L0_attn_x']
    _d['L0_attn_x'] = jax.random.normal(jax.random.fold_in(jax.random.key(seed), 1), (16, 256, 128), dtype=_x0.dtype)
    del _x0
    return _d

def reference(L0_attn_x, L0_attn_Wq, L0_attn_bq, L0_attn_Wk, L0_attn_bk, L0_attn_Wv, L0_attn_bv, L0_attn_Wo, L0_attn_bo, L0_attn_nrope_freq, L0_ffn_W, L0_ffn_Wp, L0_ffn_bp, L0_ffn_sim, L0_ffn_temp, L0_ffn_Wd0, L0_ffn_Wu0, L0_ffn_Wd1, L0_ffn_Wu1, L0_ffn_Wd2, L0_ffn_Wu2, L0_ffn_Wd3, L0_ffn_Wu3):

    def _L0_attn_ref(x, Wq, bq, Wk, bk, Wv, bv, Wo, bo, nrope_freq):
        import jax, jax.numpy as jnp
        import numpy as np
        BASE_FREQUENCY = 10000.0
        LRP = 17
        MIN_L = 1.0 - LRP / 100.0
        SDT_L = (BASE_FREQUENCY - MIN_L * BASE_FREQUENCY) * 2.0
        ARM_ATTENTION = 2.0
        HEADS_DIM = 64

        def _nrope(xs, base, angle_range):
            N, T, d = xs.shape
            half = d // 2
            inv_freq = base ** (-jnp.arange(half, dtype=jnp.float32) / half)
            pos = jnp.arange(T, dtype=jnp.float32)
            scale = angle_range / jnp.maximum(T - 1, 1)
            ang = pos[:, None] * inv_freq[None, :] * scale
            cos, sin = (jnp.cos(ang), jnp.sin(ang))
            x1, x2 = (xs[..., :half], xs[..., half:])
            return jnp.concatenate([x1 * cos - x2 * sin, x1 * sin + x2 * cos], axis=-1)
        B, T, E = x.shape
        HD = HEADS_DIM
        H = E // HD
        half = HD // 2
        q = (x @ Wq + bq).reshape(B, T, H, HD).transpose(0, 2, 1, 3)
        k = (x @ Wk + bk).reshape(B, T, H, HD).transpose(0, 2, 1, 3)
        v = (x @ Wv + bv).reshape(B, T, H, HD).transpose(0, 2, 1, 3)
        q_content, q_spatial = (q[..., :half], q[..., half:])
        k_content, k_spatial = (k[..., :half], k[..., half:])
        base = jax.nn.sigmoid(nrope_freq[0]) * SDT_L + MIN_L * BASE_FREQUENCY
        rng = ARM_ATTENTION * jnp.pi
        q_spatial = _nrope(q_spatial.reshape(B * H, T, half), base, rng).reshape(B, H, T, half)
        k_spatial = _nrope(k_spatial.reshape(B * H, T, half), base, rng).reshape(B, H, T, half)
        q = jnp.concatenate([q_content, q_spatial], axis=-1)
        k = jnp.concatenate([k_content, k_spatial], axis=-1)
        score = jnp.einsum('bhqd,bhkd->bhqk', q, k) / jnp.sqrt(jnp.float32(HD))
        attn = jax.nn.softmax(score, axis=-1)
        out = jnp.einsum('bhqk,bhkd->bhqd', attn, v)
        out = out.transpose(0, 2, 1, 3).reshape(B, T, E)
        return out @ Wo + bo

    def _L0_ffn_ref(x, W, Wp, bp, sim, temp, Wd0, Wu0, Wd1, Wu1, Wd2, Wu2, Wd3, Wu3):
        import jax, jax.numpy as jnp
        import numpy as np
        B, C, D, O = (4, 512, 128, 128)
        PROJ = 32
        RANKS = [1, 2, 4, 8]
        E = len(RANKS)
        CLAMP_MAX = float(np.log(1.0 / 0.01))

        def _l2norm(v, axis):
            return v / jnp.maximum(jnp.linalg.norm(v, axis=axis, keepdims=True), 1e-12)
        base = jnp.einsum('bcd,od->bco', x, W)
        xf = x.reshape(-1, x.shape[-1])
        proj = _l2norm(xf @ Wp.T + bp, axis=1)
        simn = _l2norm(sim, axis=0)
        scale = jnp.exp(jnp.minimum(temp, CLAMP_MAX))
        logits = proj @ simn * scale
        lw = jax.nn.softmax(logits, axis=1)
        top1 = jnp.argmax(lw, axis=1)
        ret = jnp.where(jnp.arange(E)[None, :] == top1[:, None], lw, 0.0)
        ret = ret.reshape(x.shape[0], x.shape[1], E)
        downs = (Wd0, Wd1, Wd2, Wd3)
        ups = (Wu0, Wu1, Wu2, Wu3)
        l = jnp.stack([jnp.einsum('bcr,or->bco', jnp.einsum('bcd,rd->bcr', x, d), u) for d, u in zip(downs, ups)], axis=2)
        res = jnp.sum(ret[..., None] * l, axis=2)
        return base + res
    x = L0_attn_x
    x = x + _layernorm(_L0_attn_ref(_layernorm(x, axis=-1), L0_attn_Wq, L0_attn_bq, L0_attn_Wk, L0_attn_bk, L0_attn_Wv, L0_attn_bv, L0_attn_Wo, L0_attn_bo, L0_attn_nrope_freq), axis=-1)
    x = x + _layernorm(_L0_ffn_ref(_layernorm(x, axis=-1), L0_ffn_W, L0_ffn_Wp, L0_ffn_bp, L0_ffn_sim, L0_ffn_temp, L0_ffn_Wd0, L0_ffn_Wu0, L0_ffn_Wd1, L0_ffn_Wu1, L0_ffn_Wd2, L0_ffn_Wu2, L0_ffn_Wd3, L0_ffn_Wu3), axis=-1)
    return x

_drawn_inputs = setup_inputs


def setup_inputs(seed=0):
    import zlib

    import numpy as np

    out = dict(_drawn_inputs(seed))
    spreads = {'L0_attn_bq': (0.0, 0.8),
     'L0_attn_bk': (0.0, 0.8),
     'L0_attn_bv': (0.0, 0.1),
     'L0_attn_bo': (0.0, 0.1),
     'L0_ffn_bp': (0.0, 0.8)}
    factors = {'L0_attn_Wq': 8.0,
     'L0_attn_Wk': 8.0,
     'L0_ffn_Wp': 3.399,
     'L0_ffn_sim': 3.361,
     'L0_ffn_Wd0': 4.124,
     'L0_ffn_Wu0': 3.785,
     'L0_ffn_Wd1': 4.834,
     'L0_ffn_Wu1': 3.637,
     'L0_ffn_Wd2': 8.0,
     'L0_ffn_Wu2': 8.0,
     'L0_ffn_Wd3': 8.0,
     'L0_ffn_Wu3': 21.99}
    for name, (base, spread) in spreads.items():
        noise = np.random.default_rng([zlib.crc32(name.encode()), seed]).standard_normal(out[name].shape)
        drawn = base * np.exp(spread * noise) if base else spread * noise
        out[name] = jnp.asarray(drawn.astype(out[name].dtype))
    for name, factor in factors.items():
        out[name] = (out[name] * factor).astype(out[name].dtype)
    return out
```

```python
import math

import numpy as np

import concourse.bass as bass
from concourse import mybir
from concourse.alu_op_type import AluOpType as ALU
from contextlib import ExitStack

F32 = mybir.dt.float32
BF16 = mybir.dt.bfloat16
ACT = mybir.ActivationFunctionType
AX = mybir.AxisListType

B, T, E = 16, 256, 128
P = 128
HEADS, HD = 2, 64
ROT = 16
TILES = T // P
PAIRS = B // 2
PT = 2 * TILES
UNITS = 4
VW = HD + 1
STEPS = PAIRS + 4
RANKS = [1, 2, 4, 8]
EXPERTS = len(RANKS)
RANK = sum(RANKS)
FIRST = [sum(RANKS[:e]) for e in range(EXPERTS)]
PROJ = 32
RW = PROJ + 2 * RANK
QK_SCALE = HD ** -0.5
EPS = 1e-5
CLAMP_MAX = float(np.log(1.0 / 0.01))
BASE_SPAN, BASE_LOW = 3400.0, 8300.0
ANGLE_STEP = 2.0 * math.pi / (T - 1)


def layer(nc, x, wq, bq, wk, bk, wv, bv, wo, bo, freq, w, wp, bp, sim, temp, wds, wus, out):
    x_d = x.rearrange("b (p j) d -> p b (j d)", j=TILES)
    out_d = out.rearrange("b (p j) d -> p b (j d)", j=TILES)
    ctx = ExitStack()
    with ctx:
        def sb(name, shape, dt=F32):
            return ctx.enter_context(nc.sbuf_tensor(name, shape, dt))

        def bank(name):
            return ctx.enter_context(nc.psum_tensor(name, [P, 512], F32))

        def sem(name):
            return ctx.enter_context(nc.semaphore(name))

        ident = sb("ident", [P, P])
        ones = sb("ones", [P, P])
        ones_bf = sb("ones_bf", [P, P], BF16)
        power = sb("power", [P, PT])
        w_qkv = sb("w_qkv", [P, 3 * E])
        wo_raw = sb("wo_raw", [P, E])
        wo_c = sb("wo_c", [P, E])
        w_raw = sb("w_raw", [P, E])
        w_t = sb("w_t", [P, E])
        wpd_raw = sb("wpd_raw", [PROJ + RANK, E])
        w_router = sb("w_router", [P, RW])
        wu_raw = sb("wu_raw", [P, PT, 32])
        wu_block = sb("wu_block", [P, PT, E])
        sim_raw = sb("sim_raw", [PROJ, EXPERTS])
        sim_sq = sb("sim_sq", [PROJ, EXPERTS])
        sim_n = sb("sim_n", [PROJ, EXPERTS])
        sim_r = sb("sim_r", [PROJ, RANK])
        heat = sb("heat", [PROJ, 2])
        bp_col = sb("bp_col", [PROJ, 1])
        BQ, BO, BR = 0, 3 * E, 4 * E
        bias = sb("bias", [1, 4 * E + RW])
        part = sb("part", [1, 2, 4 * E + RW])
        part_bf = sb("part_bf", [1, 2, 4 * E + RW], BF16)
        bias_qkv = sb("bias_qkv", [P, 3 * E], BF16)
        bias_o = sb("bias_o", [P, PT, E], BF16)
        bias_r = sb("bias_r", [P, PT, RW], BF16)
        mean_w = sb("mean_w", [P, 4])
        freq_c = sb("freq_c", [P, 4])
        pos = sb("pos", [P, TILES])
        expo = sb("expo", [P, ROT])
        inv_freq = sb("inv_freq", [P, ROT])
        angle = sb("angle", [P, 4, TILES, ROT])
        waves = sb("waves", [P, 2, TILES, ROT])
        cos_x = sb("cos_x", [P, TILES, 4, 2, ROT])
        sin_x = sb("sin_x", [P, TILES, 4, 2, ROT])
        code = sb("code", [P, RANK])
        share = sb("share", [P, RANK])

        x_all = sb("x_all", [P, B * T])
        v_all = sb("v_all", [P, B * TILES * HEADS * VW])
        stats1, tmp1, ve1, rs1 = sb("stats1", [P, PT, 6]), sb("tmp1", [P, 3, PT]), sb("ve1", [P, PT]), sb("rs1", [P, PT])
        statsy, tmpy, vey, rsy = sb("statsy", [P, PT, 6]), sb("tmpy", [P, 3, PT]), sb("vey", [P, PT]), sb("rsy", [P, PT])
        stats2, tmp2, ve2, rs2 = sb("stats2", [P, PT, 6]), sb("tmp2", [P, 3, PT]), sb("ve2", [P, PT]), sb("rs2", [P, PT])
        statsz, tmpz, vez, rsz = sb("statsz", [P, PT, 6]), sb("tmpz", [P, 3, PT]), sb("vez", [P, PT]), sb("rsz", [P, PT])
        mean1, nm1, mean2, nm2 = sb("mean1", [P, PT]), sb("nm1", [P, PT]), sb("mean2", [P, PT]), sb("nm2", [P, PT])
        xn = sb("xn", [P, PT, E])
        xn_t = sb("xn_t", [P, PT, P])
        qk = sb("qk", [P, PT, 4, HD])
        turn = sb("turn", [P, TILES * 4, 2, ROT])
        qk_t = sb("qk_t", [P, 2, 2, T])
        neg_max = sb("neg_max", [P, 2, TILES])
        probs = sb("probs", [P, 2, TILES, T])
        probs_t = sb("probs_t", [P, 2, TILES, T])
        den = sb("den", [P, TILES])
        heads = sb("heads", [P, PT, E])
        heads_t = sb("heads_t", [P, PT, P])
        x2n = sb("x2n", [P, PT, E])
        x2n_t = sb("x2n_t", [P, PT, P])
        route = sb("route", [P, PT, RW])
        proj_sq = sb("proj_sq", [P, PT, PROJ])
        norm2 = sb("norm2", [P, PT])
        inv_norm = sb("inv_norm", [P, PT])
        top = sb("top", [P, PT])
        below = sb("below", [P, PT, RANK])
        logit = sb("logit", [P, PT, RANK])
        expl = sb("expl", [P, PT, RANK])
        total = sb("total", [P, PT])
        key = sb("key", [P, PT, RANK])
        key_top = sb("key_top", [P, PT])
        picked = sb("picked", [P, PT, RANK])
        gated = sb("gated", [P, PT, 32])
        gated_t = sb("gated_t", [P, P])

        ps_s = [bank("ps_s0"), bank("ps_s1")]
        ps_p = bank("ps_p")
        ps_o = bank("ps_o")
        ps_q = bank("ps_q")
        ps_m = bank("ps_m")
        ps_n = bank("ps_n")
        ps_z = bank("ps_z")

        x_loaded = sem("x_loaded")
        stored = sem("stored")
        qkv_loaded, post_loaded = sem("qkv_loaded"), sem("post_loaded")
        wu_loaded, rope_loaded = sem("wu_loaded"), sem("rope_loaded")
        pool_consts, dve_consts = sem("pool_consts"), sem("dve_consts")
        rope_link, rope_angles, rope_waves = sem("rope_link"), sem("rope_angles"), sem("rope_waves")
        inv_ready = sem("inv_ready")
        front_ready, tables_ready = sem("front_ready"), sem("tables_ready")
        bias_link = sem("bias_link")
        post_mm, post_dve, post_link = sem("post_mm"), sem("post_dve"), sem("post_link")
        heat_ready, sim_norm, post_ready = sem("heat_ready"), sem("sim_norm"), sem("post_ready")
        link1, var1, rstd1, pool1 = sem("link1"), sem("var1"), sem("rstd1"), sem("pool1")
        xn_ready = sem("xn_ready")
        xt_done, xt_out = sem("xt_done"), sem("xt_out")
        qkv_done, qkv_out = sem("qkv_done"), sem("qkv_out")
        rope_mid, rope_done = sem("rope_mid"), sem("rope_done")
        qkt_done, qkt_out = sem("qkt_done"), sem("qkt_out")
        scores_done = sem("scores_done")
        max_ready, probs_ready = sem("max_ready"), sem("probs_ready")
        pt_done, pt_out = sem("pt_done"), sem("pt_out")
        pv_done, den_ready, heads_ready = sem("pv_done"), sem("den_ready"), sem("heads_ready")
        ot_done, ot_out = sem("ot_done"), sem("ot_out")
        y_done, linky, vary, rstdy = sem("y_done"), sem("linky"), sem("vary"), sem("rstdy")
        x2_ready = sem("x2_ready")
        link2, var2, rstd2, pool2 = sem("link2"), sem("var2"), sem("rstd2"), sem("pool2")
        x2n_ready = sem("x2n_ready")
        x2t_done, x2t_out = sem("x2t_done"), sem("x2t_out")
        r_done, r_out = sem("r_done"), sem("r_out")
        norm_ready, inv_norm_ready = sem("norm_ready"), sem("inv_norm_ready")
        logits_ready, exps_ready = sem("logits_ready"), sem("exps_ready")
        route_link, gated_ready = sem("route_link"), sem("gated_ready")
        dt_done, dt_out = sem("dt_done"), sem("dt_out")
        z_done, linkz, varz, rstdz = sem("z_done"), sem("linkz"), sem("varz"), sem("rstdz")
        out_ready = sem("out_ready")

        def on(s, lag):
            return not isinstance(s, int) or 0 <= s - lag < PAIRS

        def past(n, k):
            return not isinstance(n, int) or n >= k

        def rows(n, t=0, tiles=1):
            return bass.ds(n * (PT * E) + t * E, tiles * E)

        block = ctx.enter_context(nc.Block())

        @block.sync
        def _(sp):
            sp.dma_start(x_all[:, 0:2 * T].rearrange("p (b c) -> p b c", b=2), x_d[:, 0:2, :]).then_inc(x_loaded, 16)
            sp.dma_start(freq_c[:, 0:1], freq.partition_broadcast(P)).then_inc(rope_loaded, 16)
            with sp.Fori(1, PAIRS) as n:
                sp.wait_ge(x_loaded, n * 16)
                sp.dma_start(x_all[:, bass.ds(n * (2 * T), 2 * T)].rearrange("p (b c) -> p b c", b=2),
                             x_d[:, bass.ds(n * 2, 2), :]).then_inc(x_loaded, 16)
            with sp.Fori(0, PAIRS) as n:
                sp.wait_ge(out_ready, n + 1)
                sp.dma_start(out_d[:, bass.ds(n * 2, 2), :],
                             x_all[:, bass.ds(n * (2 * T), 2 * T)].rearrange("p (b c) -> p b c", b=2)).then_inc(stored, 16)
            sp.wait_ge(stored, 16 * PAIRS)

        @block.gpsimd
        def _(pool):
            pool.memset(ident[:, :], 0.0).then_inc(pool_consts, 1)
            pool.iota(pos[:, :], pattern=[[1, TILES]], base=0, channel_multiplier=TILES,
                      allow_small_or_imprecise_dtypes=True).then_inc(rope_link, 1)
            pool.iota(expo[:, :], pattern=[[1, ROT]], base=0, channel_multiplier=0,
                      allow_small_or_imprecise_dtypes=True).then_inc(rope_link, 1)
            pool.wait_ge(pool_consts, 1)
            pool.affine_select(out=ident[:, :], in_=ident[:, :], compare_op=ALU.not_equal, fill=1.0,
                               base=0, pattern=[[-1, P]], channel_multiplier=1).then_inc(pool_consts, 1)
            pool.memset(power[:, :], -0.5).then_inc(pool_consts, 1)
            pool.memset(v_all[:, :], 1.0).then_inc(pool_consts, 1)
            pool.memset(wu_raw[:, :, :], 0.0).then_inc(pool_consts, 1)
            pool.memset(gated[:, :, :], 0.0).then_inc(pool_consts, 1)
            pool.memset(wu_block[:, :, :], 0.0).then_inc(pool_consts, 1)
            for r, wu in enumerate(wus):
                if r == 0:
                    pool.wait_ge(pool_consts, 7)
                pool.dma_start(wu_raw[:, 0, FIRST[r]:FIRST[r] + RANKS[r]], wu).then_inc(wu_loaded, 16)

            def rope(n, b):
                pool.wait_ge(qkv_out, n * 4 + 2 * b + 2)
                g = qk[:, 2 * b:2 * b + 2, :, :].rearrange("p t g c -> p (t g) c")
                spatial = g[:, :, 2 * ROT:4 * ROT]
                swapped = spatial.rearrange("p g (h i) -> p g h i", h=2)[:, :, ::-1, :]
                pool.tensor_tensor(turn[:, :, :, :], swapped,
                                   sin_x[:, :, :, :, :].rearrange("p t g h i -> p (t g) h i"), ALU.mult).then_inc(rope_mid, 1)
                pool.wait_ge(rope_mid, n * 4 + 2 * b + 1)
                pool.tensor_tensor(spatial, spatial,
                                   cos_x[:, :, :, :, :].rearrange("p t g h i -> p (t g) (h i)"), ALU.mult).then_inc(rope_mid, 1)
                pool.wait_ge(rope_mid, n * 4 + 2 * b + 2)
                pool.tensor_tensor(spatial, spatial,
                                   turn[:, :, :, :].rearrange("p g h i -> p g (h i)"), ALU.add).then_inc(rope_done, 1)

            def norm_rows(n, mean, ve, rs, nm, var, link, done):
                pool.wait_ge(var, n + 1)
                pool.tensor_tensor(rs[:, :], ve[:, :], power[:, :], ALU.pow).then_inc(link, 1)
                pool.wait_ge(link, n + 1)
                pool.tensor_tensor(nm[:, :], mean[:, :], rs[:, :], ALU.mult).then_inc(done, 1)

            def step(s):
                e, f, c, d = s, s - 1, s - 3, s - 4
                if on(s, 4):
                    pool.wait_ge(norm_ready, d + 1)
                    pool.tensor_tensor(inv_norm[:, :], norm2[:, :], power[:, :], ALU.pow).then_inc(inv_norm_ready, 1)
                if on(s, 3):
                    pool.wait_ge(vary, c + 1)
                    pool.tensor_tensor(rsy[:, :], vey[:, :], power[:, :], ALU.pow).then_inc(rstdy, 1)
                if on(s, 1):
                    if isinstance(s, int) and s == 1:
                        pool.wait_ge(tables_ready, 4)
                    rope(f, 0)
                if on(s, 3):
                    if past(c, 1):
                        pool.wait_ge(x2n_ready, c)
                    norm_rows(c, mean2, ve2, rs2, nm2, var2, pool2, rstd2)
                if on(s, 4):
                    pool.wait_ge(varz, d + 1)
                    pool.tensor_tensor(rsz[:, :], vez[:, :], power[:, :], ALU.pow).then_inc(rstdz, 1)
                if on(s, 0):
                    if past(e, 1):
                        pool.wait_ge(xn_ready, e)
                    norm_rows(e, mean1, ve1, rs1, nm1, var1, pool1, rstd1)
                if on(s, 1):
                    rope(f, 1)

            pool.wait_ge(pool_consts, 3)
            pool.wait_ge(rope_link, 6)
            pool.tensor_tensor(inv_freq[:, :], freq_c[:, 3:4].to_broadcast([P, ROT]), expo[:, :], ALU.pow).then_inc(inv_ready, 1)
            step(0)
            step(1)
            pool.wait_ge(post_link, 4)
            pool.tensor_tensor(sim_n[:, :], sim_sq[:, :], power[0:PROJ, 0:EXPERTS], ALU.pow).then_inc(sim_norm, 1)
            for s in range(2, 4):
                step(s)
            with pool.Fori(4, PAIRS) as s:
                step(s)
            for s in range(PAIRS, STEPS):
                step(s)

        @block.scalar
        def _(act):
            for k, (wt, bb) in enumerate(((wq, bq), (wk, bk), (wv, bv))):
                act.dma_start(w_qkv[:, k * E:(k + 1) * E], wt).then_inc(qkv_loaded, 16)
                act.dma_start(bias[0:1, BQ + k * E:BQ + (k + 1) * E], bb.partition_broadcast(1)).then_inc(qkv_loaded, 16)
            for dst, src in ((wo_raw[:, :], wo), (bias[0:1, BO:BO + E], bo.partition_broadcast(1)), (w_raw[:, :], w),
                             (wpd_raw[0:PROJ, :], wp), (bias[0:1, BR:BR + PROJ], bp.partition_broadcast(1)),
                             (bp_col[:, :], bp.rearrange("(p a) -> p a", a=1)), (sim_raw[:, :], sim),
                             (heat[:, 0:1], temp.partition_broadcast(PROJ))):
                act.dma_start(dst, src).then_inc(post_loaded, 16)
            for r, wd in enumerate(wds):
                act.dma_start(wpd_raw[PROJ + FIRST[r]:PROJ + FIRST[r] + RANKS[r], :], wd).then_inc(post_loaded, 16)
            act.wait_ge(rope_loaded, 16)
            act.activation(freq_c[:, 1:2], freq_c[:, 0:1], ACT.Exp, scale=-1.0).then_inc(rope_link, 1)
            act.wait_ge(rope_angles, 1)
            act.activation(waves[:, :, :, :], angle[:, 2:4, :, :], ACT.Sin).then_inc(rope_waves, 1)

            def exps(n, u):
                act.wait_ge(max_ready, n * 4 + u + 1)
                if past(n, 1) or u >= 2:
                    act.wait_ge(pt_done, n * 4 + u - 1)
                for j in range(TILES):
                    last = act.activation(probs[:, u % 2, j, :], ps_s[u % 2][:, j * T:(j + 1) * T], ACT.Exp,
                                          bias=neg_max[:, u % 2, j:j + 1])
                last.then_inc(probs_ready, 1)

            def qkt(n, b):
                act.wait_ge(qkt_done, n * 2 + b + 1)
                if past(n, 1):
                    act.wait_ge(scores_done, n * 4 + 2 * b - 2)
                act.activation(qk_t[:, b, :, :], ps_m[:, :].rearrange("p (a t) -> p a t", a=2), ACT.Copy).then_inc(qkt_out, 1)

            def probs_turned(n, u):
                act.wait_ge(pt_done, n * 4 + u + 1)
                if past(n, 1) or u >= 2:
                    act.wait_ge(pv_done, n * 4 + u - 1)
                act.activation(probs_t[:, u % 2, :, :], ps_p[:, :].rearrange("p (a t) -> p a t", a=TILES), ACT.Copy).then_inc(pt_out, 1)

            def qkv(n, t):
                act.wait_ge(qkv_done, n * 4 + t + 1)
                if past(n, 1):
                    act.wait_ge(qkt_done, n * 2 + t // 2 - 1)
                act.activation(qk[:, t, :, :].rearrange("p g c -> p (g c)"), ps_q[:, 0:2 * E], ACT.Copy)
                if isinstance(n, int) and n == 0 and t == 0:
                    act.wait_ge(pool_consts, 4)
                act.activation(v_all[:, bass.ds(n * (PT * HEADS * VW) + t * HEADS * VW, HEADS * VW)]
                               .rearrange("p (h c) -> p h c", h=HEADS)[:, :, 0:HD],
                               ps_q[:, 2 * E:3 * E].rearrange("p (h c) -> p h c", h=HEADS), ACT.Copy).then_inc(qkv_out, 1)

            def normalise(n, dst, rs, nm, ready):
                for t in range(PT):
                    last = act.activation(dst[:, t, :], x_all[:, rows(n, t)], ACT.Identity,
                                          bias=nm[:, t:t + 1], scale=rs[:, t:t + 1])
                last.then_inc(ready, 1)

            def step(s):
                e, f, a, c, d = s, s - 1, s - 2, s - 3, s - 4
                if on(s, 2):
                    exps(a, 0)
                if on(s, 3):
                    act.wait_ge(ot_done, c + 1)
                    if past(c, 1):
                        act.wait_ge(y_done, c)
                    act.activation(heads_t[:, :, :].rearrange("p t c -> p (t c)"), ps_z[:, :], ACT.Copy).then_inc(ot_out, 1)
                if on(s, 2):
                    qkt(a, 1)
                if on(s, 1):
                    act.wait_ge(xt_done, f + 1)
                    if past(f, 1):
                        act.wait_ge(qkv_done, f * 4)
                    act.activation(xn_t[:, :, :].rearrange("p t c -> p (t c)"), ps_n[:, :], ACT.Copy).then_inc(xt_out, 1)
                if on(s, 2):
                    probs_turned(a, 0)
                if on(s, 4):
                    act.wait_ge(logits_ready, d + 1)
                    act.activation(expl[:, :, :], logit[:, :, :], ACT.Exp).then_inc(exps_ready, 1)
                if on(s, 2):
                    exps(a, 1)
                if on(s, 1):
                    qkv(f, 0)
                if on(s, 2):
                    probs_turned(a, 1)
                if on(s, 1):
                    qkv(f, 1)
                if on(s, 4):
                    act.wait_ge(dt_done, d + 1)
                    if past(d, 1):
                        act.wait_ge(z_done, d)
                    act.activation(gated_t[:, :], ps_n[:, 0:P], ACT.Copy).then_inc(dt_out, 1)
                if on(s, 2):
                    exps(a, 2)
                if on(s, 1):
                    qkv(f, 2)
                if on(s, 2):
                    probs_turned(a, 2)
                if on(s, 3):
                    act.wait_ge(rstd2, c + 1)
                    if past(c, 1):
                        act.wait_ge(x2t_done, c)
                    normalise(c, x2n, rs2, nm2, x2n_ready)
                if on(s, 2):
                    exps(a, 3)
                if on(s, 1):
                    qkv(f, 3)
                if on(s, 2):
                    probs_turned(a, 3)
                if on(s, 1):
                    qkt(f, 0)
                if on(s, 3):
                    act.wait_ge(x2t_done, c + 1)
                    if past(c, 1):
                        act.wait_ge(z_done, c)
                    act.activation(x2n_t[:, :, :].rearrange("p t c -> p (t c)"), ps_n[:, :], ACT.Copy).then_inc(x2t_out, 1)
                if on(s, 0):
                    act.wait_ge(rstd1, e + 1)
                    if past(e, 1):
                        act.wait_ge(xt_done, e)
                    normalise(e, xn, rs1, nm1, xn_ready)
                if on(s, 3):
                    act.wait_ge(r_done, c + 1)
                    if past(c, 1):
                        act.wait_ge(gated_ready, c)
                    act.activation(route[:, :, :].rearrange("p t c -> p (t c)"), ps_q[:, 0:PT * RW], ACT.Copy)
                    act.activation(proj_sq[:, :, :],
                                   ps_q[:, 0:PT * RW].rearrange("p (t c) -> p t c", t=PT)[:, :, 0:PROJ],
                                   ACT.Square).then_inc(r_out, 1)

            step(0)
            step(1)
            act.wait_ge(post_link, 3)
            act.activation(heat[:, 0:1], heat[:, 1:2], ACT.Exp).then_inc(heat_ready, 1)
            for s in range(2, 4):
                step(s)
            with act.Fori(4, PAIRS) as s:
                step(s)
            for s in range(PAIRS, STEPS):
                step(s)

        @block.vector
        def _(dve):
            dve.memset(ones_bf[:, :], 1.0).then_inc(dve_consts, 1)
            dve.memset(ones[:, :], 1.0).then_inc(dve_consts, 1)
            dve.memset(bias_qkv[:, :].bitcast(F32), 0.0).then_inc(dve_consts, 1)
            dve.memset(bias_o[:, :, :].rearrange("p t c -> p (t c)").bitcast(F32), 0.0).then_inc(dve_consts, 1)
            dve.memset(bias_r[:, :, :].rearrange("p t c -> p (t c)").bitcast(F32), 0.0).then_inc(dve_consts, 1)
            for x_, r in enumerate(RANKS):
                dve.memset(code[:, FIRST[x_]:FIRST[x_] + r], float(EXPERTS - x_)).then_inc(dve_consts, 1)
                dve.memset(share[:, FIRST[x_]:FIRST[x_] + r], 1.0 / r).then_inc(dve_consts, 1)

            links = {}

            def link(ins, chain, least=0):
                links[chain] = max(links.get(chain, 0), least) + 1
                ins.then_inc(chain, 1)
                dve.wait_ge(chain, links[chain])

            dve.wait_ge(rope_link, 3)
            links[rope_link] = 3
            link(dve.tensor_scalar(freq_c[:, 2:3], freq_c[:, 1:2], 1.0, None, ALU.add), rope_link)
            link(dve.reciprocal(freq_c[:, 2:3], freq_c[:, 2:3]), rope_link)
            dve.tensor_scalar(expo[:, :], expo[:, :], -1.0 / ROT, None, ALU.mult)
            link(dve.tensor_scalar(freq_c[:, 3:4], freq_c[:, 2:3], BASE_SPAN, BASE_LOW, ALU.mult, ALU.add), rope_link)
            dve.wait_ge(qkv_loaded, 96)
            dve.tensor_scalar(w_qkv[:, 0:E], w_qkv[:, 0:E], QK_SCALE, None, ALU.mult).then_inc(front_ready, 1)
            link(dve.tensor_scalar(bias[:, 0:E], bias[:, 0:E], QK_SCALE, None, ALU.mult), bias_link)

            def split(at, n, outs):
                b, r1, r2 = bias[:, at:at + n], part[:, 0, at:at + n], part[:, 1, at:at + n]
                hi, mid = part_bf[:, 0, at:at + n], part_bf[:, 1, at:at + n]
                link(dve.tensor_copy(hi, b), bias_link)
                link(dve.tensor_tensor(r1, b, hi, ALU.subtract), bias_link)
                link(dve.tensor_copy(mid, r1), bias_link)
                link(dve.tensor_tensor(r2, r1, mid, ALU.subtract), bias_link)
                for row, src in ((0, hi), (32, mid), (64, r2)):
                    last = dve.tensor_copy(outs(row), src if len(outs(row).shape) == 2
                                           else src.unsqueeze(1).to_broadcast([1, PT, n]))
                return last

            split(BQ, 3 * E, lambda r: bias_qkv[r:r + 1, :]).then_inc(front_ready, 1)

            dve.wait_ge(inv_ready, 1)
            for j in range(TILES):
                last = dve.tensor_scalar(angle[:, 0, j, :], inv_freq[:, :], pos[:, j:j + 1], ANGLE_STEP, ALU.mult, ALU.mult)
            link(last, rope_link, 6)
            link(dve.tensor_scalar(angle[:, 1, :, :], angle[:, 0, :, :], -math.pi, None, ALU.add), rope_link)
            lim = 3.1415925
            link(dve.tensor_scalar(angle[:, 2, :, :], angle[:, 1, :, :], lim, -lim, ALU.min, ALU.max), rope_link)
            link(dve.tensor_scalar(angle[:, 1, :, :], angle[:, 2, :, :], -1.0, None, ALU.mult), rope_link)
            link(dve.tensor_tensor(angle[:, 0, :, :], angle[:, 1, :, :], angle[:, 2, :, :], ALU.max), rope_link)
            dve.tensor_scalar(angle[:, 3, :, :], angle[:, 0, :, :], -1.0, math.pi / 2, ALU.mult, ALU.add).then_inc(rope_angles, 1)

            def tile_stats(src, stats):
                for t in range(PT):
                    last = dve.bn_stats(stats[:, t, :], src(t))
                return last

            def variance(n, stats, tmp, ve, link_, var, rstd, mean=None):
                gap, dev, gap2 = tmp[:, 0, :], tmp[:, 1, :], tmp[:, 2, :]
                if past(n, 1):
                    dve.wait_ge(rstd, n)
                dve.wait_ge(link_, n * 3 + 1)
                dve.tensor_tensor(gap, stats[:, :, 1], stats[:, :, 4], ALU.subtract).then_inc(link_, 1)
                dve.scalar_tensor_tensor(dev, stats[:, :, 2], EPS * E, stats[:, :, 5], ALU.add, ALU.add)
                dve.wait_ge(link_, n * 3 + 2)
                if mean is not None:
                    dve.scalar_tensor_tensor(mean[:, :], gap, -0.5, stats[:, :, 4], ALU.mult, ALU.subtract)
                dve.scalar_tensor_tensor(gap2, gap, 0.25, gap, ALU.mult, ALU.mult).then_inc(link_, 1)
                dve.wait_ge(link_, n * 3 + 3)
                dve.scalar_tensor_tensor(ve[:, :], dev, 1.0 / E, gap2, ALU.mult, ALU.add).then_inc(var, 1)

            def row_max(n, u):
                dve.wait_ge(scores_done, n * 4 + u + 1)
                dve.tensor_reduce(neg_max[:, u % 2, :], ps_s[u % 2][:, :].rearrange("p (j k) -> p j k", j=TILES),
                                  AX.X, ALU.max, negate=True).then_inc(max_ready, 1)

            def divide(n, u):
                o = ps_o[:, 0:TILES * VW].rearrange("p (j c) -> p j c", j=TILES)
                b, h = u // 2, u % 2
                dve.wait_ge(pv_done, n * 4 + u + 1)
                dve.reciprocal(den[:, :], o[:, :, HD]).then_inc(den_ready, 1)
                if u == 0 and past(n, 1):
                    dve.wait_ge(ot_done, n)
                dve.wait_ge(den_ready, n * 4 + u + 1)
                dve.tensor_tensor(heads[:, 2 * b:2 * b + 2, h * HD:(h + 1) * HD], o[:, :, 0:HD],
                                  den[:, :].unsqueeze(2).to_broadcast([P, TILES, HD]), ALU.mult).then_inc(heads_ready, 1)

            def route_a(n):
                k = n * 9
                dve.wait_ge(r_out, n + 1)
                dve.tensor_reduce(norm2[:, :], proj_sq[:, :, :], AX.X, ALU.add).then_inc(route_link, 1)
                dve.tensor_reduce(top[:, :], route[:, :, PROJ + RANK:RW], AX.X, ALU.max).then_inc(route_link, 1)
                dve.wait_ge(route_link, k + 1)
                dve.tensor_scalar(norm2[:, :], norm2[:, :], 1e-24, None, ALU.max).then_inc(norm_ready, 1)
                dve.wait_ge(route_link, k + 2)
                dve.tensor_tensor(below[:, :, :], route[:, :, PROJ + RANK:RW],
                                  top[:, :].unsqueeze(2).to_broadcast([P, PT, RANK]), ALU.subtract).then_inc(route_link, 1)
                dve.wait_ge(route_link, k + 3)
                dve.scalar_tensor_tensor(key[:, :, :], below[:, :, :], 0.0,
                                         code[:, :].unsqueeze(1).to_broadcast([P, PT, RANK]), ALU.is_ge, ALU.mult).then_inc(route_link, 1)
                dve.wait_ge(route_link, k + 4)
                dve.tensor_reduce(key_top[:, :], key[:, :, :], AX.X, ALU.max).then_inc(route_link, 1)
                dve.wait_ge(inv_norm_ready, n + 1)
                dve.tensor_tensor(logit[:, :, :], below[:, :, :],
                                  inv_norm[:, :].unsqueeze(2).to_broadcast([P, PT, RANK]), ALU.mult).then_inc(logits_ready, 1)

            def route_b(n):
                k = n * 9 + 5
                dve.wait_ge(route_link, k)
                dve.tensor_tensor(key[:, :, :], key[:, :, :],
                                  key_top[:, :].unsqueeze(2).to_broadcast([P, PT, RANK]), ALU.is_equal).then_inc(route_link, 1)
                dve.wait_ge(exps_ready, n + 1)
                dve.tensor_tensor(expl[:, :, :], expl[:, :, :],
                                  share[:, :].unsqueeze(1).to_broadcast([P, PT, RANK]), ALU.mult).then_inc(route_link, 1)
                dve.wait_ge(route_link, k + 2)
                dve.tensor_reduce(total[:, :], expl[:, :, :], AX.X, ALU.add).then_inc(route_link, 1)
                dve.tensor_tensor(picked[:, :, :], key[:, :, :], route[:, :, PROJ:PROJ + RANK], ALU.mult)
                dve.wait_ge(route_link, k + 3)
                dve.reciprocal(total[:, :], total[:, :]).then_inc(route_link, 1)
                dve.wait_ge(route_link, k + 4)
                if past(n, 1):
                    dve.wait_ge(dt_done, n)
                dve.tensor_tensor(gated[:, :, 0:RANK], picked[:, :, :],
                                  total[:, :].unsqueeze(2).to_broadcast([P, PT, RANK]), ALU.mult).then_inc(gated_ready, 1)

            def step(s):
                e, f, a, c, d = s, s - 1, s - 2, s - 3, s - 4
                if on(s, 4):
                    route_a(d)
                if on(s, 2):
                    row_max(a, 1)
                    divide(a, 0)
                if on(s, 3):
                    dve.wait_ge(y_done, c + 1)
                    tile_stats(lambda t: ps_m[:, t * E:(t + 1) * E], statsy).then_inc(linky, 1)
                    variance(c, statsy, tmpy, vey, linky, vary, rstdy)
                if on(s, 4):
                    route_b(d)
                if on(s, 2):
                    row_max(a, 2)
                if on(s, 3):
                    dve.wait_ge(rstdy, c + 1)
                    for t in range(PT):
                        last = dve.scalar_tensor_tensor(x_all[:, rows(c, t)], ps_m[:, t * E:(t + 1) * E], rsy[:, t:t + 1],
                                                        x_all[:, rows(c, t)], ALU.mult, ALU.add)
                    last.then_inc(x2_ready, 1)
                if on(s, 2):
                    divide(a, 1)
                if on(s, 3):
                    if not on(s, 2):
                        dve.wait_ge(x2_ready, c + 1)
                    tile_stats(lambda t: x_all[:, rows(c, t)], stats2).then_inc(link2, 1)
                    variance(c, stats2, tmp2, ve2, link2, var2, rstd2, mean2)
                if on(s, 2):
                    row_max(a, 3)
                    divide(a, 2)
                if on(s, 4):
                    dve.wait_ge(z_done, d + 1)
                    tile_stats(lambda t: ps_z[:, t * E:(t + 1) * E], statsz).then_inc(linkz, 1)
                if on(s, 0):
                    dve.wait_ge(x_loaded, e * 16 + 16)
                if on(s, 4):
                    variance(d, statsz, tmpz, vez, linkz, varz, rstdz)
                if on(s, 0):
                    tile_stats(lambda t: x_all[:, rows(e, t)], stats1).then_inc(link1, 1)
                    variance(e, stats1, tmp1, ve1, link1, var1, rstd1, mean1)
                if on(s, 4):
                    dve.wait_ge(rstdz, d + 1)
                    for t in range(PT):
                        last = dve.scalar_tensor_tensor(x_all[:, rows(d, t)], ps_z[:, t * E:(t + 1) * E], rsz[:, t:t + 1],
                                                        x_all[:, rows(d, t)], ALU.mult, ALU.add)
                    last.then_inc(out_ready, 1)
                if on(s, 2):
                    divide(a, 3)
                if on(s, 1):
                    row_max(f, 0)

            step(0)
            dve.wait_ge(rope_waves, 1)
            for h in range(2):
                dve.tensor_scalar(cos_x[:, :, :, h, :], waves[:, 1, :, :].unsqueeze(2).to_broadcast([P, TILES, 4, ROT]),
                                  -1.0, None, ALU.mult).then_inc(tables_ready, 1)
                dve.tensor_scalar(sin_x[:, :, :, h, :], waves[:, 0, :, :].unsqueeze(2).to_broadcast([P, TILES, 4, ROT]),
                                  1.0 - 2.0 * h, None, ALU.mult).then_inc(tables_ready, 1)
            step(1)

            dve.wait_ge(post_loaded, 12 * 16)
            dve.wait_ge(wu_loaded, 4 * 16)
            dve.wait_ge(pool_consts, 8 - 1)
            dve.wait_ge(dve_consts, 5 + 2 * EXPERTS)
            link(dve.tensor_tensor(sim_sq[:, :], sim_raw[:, :], sim_raw[:, :], ALU.mult), post_link)
            dve.tensor_copy(wu_raw[:, 1:PT, :], wu_raw[:, 0:1, :].to_broadcast([P, PT - 1, 32])).then_inc(post_dve, 1)
            link(dve.tensor_reduce(mean_w[:, 0:1], wo_raw[:, :], AX.X, ALU.add), post_link)
            dve.tensor_scalar(heat[:, 1:2], heat[:, 0:1], CLAMP_MAX, None, ALU.min).then_inc(post_link, 1)
            links[post_link] = 3
            dve.wait_ge(post_mm, 1)
            dve.tensor_scalar(sim_sq[:, :], ps_o[0:PROJ, 0:EXPERTS], 1e-24, None, ALU.max).then_inc(post_link, 1)
            links[post_link] = 4
            link(dve.tensor_scalar(mean_w[:, 0:1], mean_w[:, 0:1], 1.0 / E, None, ALU.mult), post_link)
            dve.tensor_scalar(wo_c[:, :], wo_raw[:, :], mean_w[:, 0:1], None, ALU.subtract).then_inc(post_dve, 1)
            dve.wait_ge(post_mm, 2)
            link(dve.tensor_reduce(mean_w[:, 1:2], ps_z[:, 0:E], AX.X, ALU.add), post_link)
            link(dve.tensor_scalar(mean_w[:, 1:2], mean_w[:, 1:2], 1.0 / E, None, ALU.mult), post_link)
            dve.tensor_scalar(w_t[:, :], ps_z[:, 0:E], mean_w[:, 1:2], None, ALU.subtract).then_inc(post_dve, 1)
            dve.wait_ge(post_mm, 3)
            dve.tensor_copy(w_router[:, 0:PROJ + RANK], ps_p[:, 0:PROJ + RANK]).then_inc(post_dve, 1)
            dve.wait_ge(sim_norm, 1)
            dve.wait_ge(heat_ready, 1)
            link(dve.tensor_tensor(sim_n[:, :], sim_raw[:, :], sim_n[:, :], ALU.mult), post_link)
            for x_, r in enumerate(RANKS):
                last = dve.tensor_scalar(sim_r[:, FIRST[x_]:FIRST[x_] + r], sim_n[:, x_:x_ + 1].to_broadcast([PROJ, r]),
                                         heat[:, 0:1], None, ALU.mult)
            last.then_inc(post_dve, 1)
            dve.wait_ge(post_mm, 4)
            link(dve.tensor_reduce(mean_w[:, 2:3], ps_z[:, 0:E], AX.X, ALU.add), post_link)
            link(dve.tensor_scalar(mean_w[:, 2:3], mean_w[:, 2:3], 1.0 / E, None, ALU.mult), post_link)
            for t in range(PT):
                rr = slice(32 * t, 32 * t + 32)
                last = dve.tensor_scalar(wu_block[rr, t, :], ps_z[rr, 0:E], mean_w[rr, 2:3], None, ALU.subtract)
            last.then_inc(post_dve, 1)
            dve.wait_ge(post_mm, 5)
            dve.tensor_copy(w_router[:, PROJ + RANK:RW], ps_p[:, 0:RANK]).then_inc(post_dve, 1)
            dve.wait_ge(post_mm, 6)
            dve.tensor_copy(bias[:, BR + PROJ + RANK:BR + RW], ps_o[0:1, 0:RANK])
            dve.memset(bias[:, BR + PROJ:BR + PROJ + RANK], 0.0)
            link(dve.tensor_reduce(mean_w[0:1, 3:4], bias[:, BO:BO + E], AX.X, ALU.add), bias_link)
            link(dve.tensor_scalar(mean_w[0:1, 3:4], mean_w[0:1, 3:4], 1.0 / E, None, ALU.mult), bias_link)
            link(dve.tensor_scalar(bias[:, BO:BO + E], bias[:, BO:BO + E], mean_w[0:1, 3:4], None, ALU.subtract), bias_link)
            split(BO, E, lambda r: bias_o[r:r + 1, :, :])
            split(BR, RW, lambda r: bias_r[r:r + 1, :, :]).then_inc(post_dve, 1)

            for s in range(2, 4):
                step(s)
            with dve.Fori(4, PAIRS) as s:
                step(s)
            for s in range(PAIRS, STEPS):
                step(s)

        @block.tensor
        def _(pe):
            def scores(n, u):
                b, h = u // 2, u % 2
                r = slice(h * HD, (h + 1) * HD)
                pe.wait_ge(qkt_out, n * 2 + b + 1)
                if past(n, 1) or u >= 2:
                    pe.wait_ge(probs_ready, n * 4 + u - 1)
                for j in range(TILES):
                    last = pe.matmul(ps_s[u % 2][:, j * T:(j + 1) * T], qk_t[r, b, 0, j * P:(j + 1) * P],
                                     qk_t[r, b, 1, :], start=True, stop=True)
                last.then_inc(scores_done, 1)

            def turn_probs(n, u):
                pe.wait_ge(probs_ready, n * 4 + u + 1)
                if past(n, 1) or u >= 1:
                    pe.wait_ge(pt_out, n * 4 + u)
                for i in range(TILES):
                    for j in range(TILES):
                        last = pe.transpose(ps_p[:, i * T + j * P:i * T + (j + 1) * P],
                                            probs[:, u % 2, j, i * P:(i + 1) * P], ident[:, :])
                last.then_inc(pt_done, 1)

            def weigh(n, u):
                b, h = u // 2, u % 2
                pe.wait_ge(pt_out, n * 4 + u + 1)
                if past(n, 1) or u >= 1:
                    pe.wait_ge(heads_ready, n * 4 + u)
                for j in range(TILES):
                    for i in range(TILES):
                        v = v_all[:, bass.ds(n * (PT * HEADS * VW) + ((2 * b + i) * HEADS + h) * VW, VW)]
                        last = pe.matmul(ps_o[:, j * VW:(j + 1) * VW], probs_t[:, u % 2, i, j * P:(j + 1) * P], v,
                                         start=(i == 0), stop=(i == TILES - 1))
                last.then_inc(pv_done, 1)

            def turn_qk(n, b):
                pe.wait_ge(rope_done, n * 2 + b + 1)
                for a in range(2):
                    for j in range(TILES):
                        last = pe.transpose(ps_m[:, a * T + j * P:a * T + (j + 1) * P],
                                            qk[:, 2 * b + j, 2 * a:2 * a + 2, :].rearrange("p g c -> p (g c)"), ident[:, :])
                last.then_inc(qkt_done, 1)

            def turn_rows(bank_, src, done):
                for t in range(PT):
                    last = pe.transpose(bank_[:, t * P:(t + 1) * P], src[:, t, :], ident[:, :])
                last.then_inc(done, 1)

            def project_qkv(n, t):
                if t > 0:
                    pe.wait_ge(qkv_out, n * 4 + t)
                pe.matmul(ps_q[:, 0:3 * E], ones_bf[:, :], bias_qkv[:, :], start=True, stop=False)
                pe.matmul(ps_q[:, 0:3 * E], xn_t[:, t, :], w_qkv[:, :], start=False, stop=True).then_inc(qkv_done, 1)

            def step(s):
                f, a, c, d = s - 1, s - 2, s - 3, s - 4
                F_, A_, C_, D_ = on(s, 1), on(s, 2), on(s, 3), on(s, 4)
                if A_:
                    scores(a, 1)
                if C_:
                    pe.wait_ge(heads_ready, c * 4 + 4)
                    if past(c, 2):
                        pe.wait_ge(out_ready, c - 1)
                    turn_rows(ps_z, heads, ot_done)
                if A_:
                    pe.wait_ge(qkt_out, a * 2 + 1)
                    turn_qk(a, 1)
                if F_:
                    pe.wait_ge(xn_ready, f + 1)
                    if past(c, 1):
                        pe.wait_ge(x2t_out, c)
                    turn_rows(ps_n, xn, xt_done)
                if A_:
                    if isinstance(s, int) and s == 2:
                        pe.wait_ge(post_dve, 8)
                    turn_probs(a, 0)
                    weigh(a, 0)
                if C_:
                    pe.wait_ge(ot_out, c + 1)
                    if A_:
                        pe.wait_ge(qkt_out, a * 2 + 2)
                    else:
                        pe.wait_ge(x2_ready, c)
                    pe.matmul(ps_m[:, :], ones_bf[:, :], bias_o[:, :, :].rearrange("p t c -> p (t c)"), start=True, stop=False)
                    for t in range(PT):
                        last = pe.matmul(ps_m[:, t * E:(t + 1) * E], heads_t[:, t, :], wo_c[:, :], start=False, stop=(t == PT - 1))
                    last.then_inc(y_done, 1)
                if A_:
                    scores(a, 2)
                if F_:
                    pe.wait_ge(xt_out, f + 1)
                    if past(c, 1):
                        pe.wait_ge(r_out, c)
                    elif past(f, 1):
                        pe.wait_ge(qkv_out, f * 4)
                    project_qkv(f, 0)
                if A_:
                    turn_probs(a, 1)
                if F_:
                    project_qkv(f, 1)
                if D_:
                    pe.wait_ge(gated_ready, d + 1)
                    if F_:
                        pe.wait_ge(xt_out, f + 1)
                    else:
                        pe.wait_ge(x2t_out, d + 1)
                    pe.transpose(ps_n[:, 0:P], gated[:, :, :].rearrange("p t c -> p (t c)"), ident[:, :]).then_inc(dt_done, 1)
                if A_:
                    weigh(a, 1)
                    scores(a, 3)
                if F_:
                    project_qkv(f, 2)
                if A_:
                    turn_probs(a, 2)
                if D_:
                    if C_:
                        pe.wait_ge(ot_out, c + 1)
                    else:
                        pe.wait_ge(out_ready, d)
                    for t in range(PT):
                        pe.matmul(ps_z[:, t * E:(t + 1) * E], x2n_t[:, t, :], w_t[:, :], start=(t == 0), stop=False)
                    pe.wait_ge(dt_out, d + 1)
                    pe.matmul(ps_z[:, :], gated_t[:, :], wu_block[:, :, :].rearrange("p t c -> p (t c)"),
                              start=False, stop=True).then_inc(z_done, 1)
                if A_:
                    weigh(a, 2)
                if F_:
                    project_qkv(f, 3)
                if A_:
                    turn_probs(a, 3)
                if F_:
                    if C_:
                        pe.wait_ge(x2_ready, c + 1)
                    elif A_:
                        pe.wait_ge(qkt_out, a * 2 + 2)
                    turn_qk(f, 0)
                if C_:
                    pe.wait_ge(x2n_ready, c + 1)
                    if D_:
                        pe.wait_ge(dt_out, d + 1)
                    elif F_:
                        pe.wait_ge(xt_out, f + 1)
                    turn_rows(ps_n, x2n, x2t_done)
                if A_:
                    weigh(a, 3)
                if C_:
                    pe.wait_ge(x2t_out, c + 1)
                    if F_:
                        pe.wait_ge(qkv_out, f * 4 + 4)
                    elif past(c, 1):
                        pe.wait_ge(r_out, c)
                    pe.matmul(ps_q[:, 0:PT * RW], ones_bf[:, :], bias_r[:, :, :].rearrange("p t c -> p (t c)"), start=True, stop=False)
                    for t in range(PT):
                        last = pe.matmul(ps_q[:, t * RW:(t + 1) * RW], x2n_t[:, t, :], w_router[:, :], start=False, stop=(t == PT - 1))
                    last.then_inc(r_done, 1)
                if F_:
                    scores(f, 0)

            pe.wait_ge(pool_consts, 2)
            pe.wait_ge(dve_consts, 2)
            pe.wait_ge(front_ready, 2)
            step(0)
            step(1)
            pe.wait_ge(post_link, 1)
            pe.matmul(ps_o[0:PROJ, 0:EXPERTS], ones[0:PROJ, 0:PROJ], sim_sq[:, :], start=True, stop=True).then_inc(post_mm, 1)
            pe.wait_ge(post_loaded, 12 * 16)
            pe.transpose(ps_z[:, 0:E], w_raw[:, :], ident[:, :]).then_inc(post_mm, 1)
            pe.transpose(ps_p[:, 0:PROJ + RANK], wpd_raw[:, :], ident[0:PROJ + RANK, 0:PROJ + RANK]).then_inc(post_mm, 1)
            pe.wait_ge(post_dve, 3)
            pe.transpose(ps_z[:, 0:E], wu_raw[:, :, :].rearrange("p t c -> p (t c)"), ident[:, :]).then_inc(post_mm, 1)
            pe.wait_ge(post_dve, 5)
            pe.matmul(ps_p[:, 0:RANK], wpd_raw[0:PROJ, :], sim_r[:, :], start=True, stop=True).then_inc(post_mm, 1)
            pe.matmul(ps_o[0:1, 0:RANK], bp_col[:, :], sim_r[:, :], start=True, stop=True).then_inc(post_mm, 1)
            for s in range(2, 4):
                step(s)
            with pe.Fori(4, PAIRS) as s:
                step(s)
            for s in range(PAIRS, STEPS):
                step(s)


_INS = (["L0_attn_x"] + [f"L0_attn_{n}" for n in ("Wq", "bq", "Wk", "bk", "Wv", "bv", "Wo", "bo", "nrope_freq")]
        + [f"L0_ffn_{n}" for n in ("W", "Wp", "bp", "sim", "temp")]
        + [f"L0_ffn_Wd{i}" for i in range(4)] + [f"L0_ffn_Wu{i}" for i in range(4)])


def kernel(**inputs):
    import concourse.bacc as bacc
    from concourse.bass_utils import run_bass_kernel_spmd

    nc = bacc.Bacc("TRN2", target_bir_lowering=False, num_devices=1)
    arrays, args = {}, []
    for name in _INS:
        a = np.ascontiguousarray(inputs[name])
        arrays[f"in_{name}"] = a
        args.append(nc.dram_tensor(f"in_{name}", a.shape, mybir.dt.from_np(a.dtype), kind="ExternalInput").ap())
    out = nc.dram_tensor("out", (B, T, E), F32, kind="ExternalOutput").ap()
    layer(nc, *args[:15], args[15:19], args[19:23], out)
    r = run_bass_kernel_spmd(nc, [arrays], core_ids=[0])
    return r.results[0]["out"]
```

```python
import math

import numpy as np

import concourse.bass as bass
from concourse import mybir
from concourse.alu_op_type import AluOpType as ALU
from contextlib import ExitStack

F32 = mybir.dt.float32
BF16 = mybir.dt.bfloat16
F32R = mybir.dt.float32r
ACT = mybir.ActivationFunctionType
AX = mybir.AxisListType

B, T, E = 16, 256, 128
P = 128
HEADS, HD = 2, 64
ROT = 16
TILES = T // P
PAIRS = B // 2
PT = 2 * TILES
UNITS = 4
VW = E + 1
VT = HEADS * VW
STEPS = PAIRS + 4
RANKS = [1, 2, 4, 8]
EXPERTS = len(RANKS)
RANK = sum(RANKS)
FIRST = [sum(RANKS[:e]) for e in range(EXPERTS)]
PROJ = 32
RW = PROJ + 2 * RANK
ZW = RW + E
BANK = 512
ROWS = 4 * E + PROJ + 2
AT_BV, AT_BO, AT_BP, AT_TEMP, AT_FREQ = 2 * E, 3 * E, 4 * E, 4 * E + PROJ, 4 * E + PROJ + 1
QK_SCALE = HD ** -0.5
EPS = 1e-5
CLAMP_MAX = float(np.log(1.0 / 0.01))
BASE_SPAN, BASE_LOW = 3400.0, 8300.0
ANGLE_STEP = 2.0 * math.pi / (T - 1)


def layer(nc, x, w_attn, vectors, w_ffn, w_down, sim, out):
    x_d = x.rearrange("b (p j) d -> p b (j d)", j=TILES)
    out_d = out.rearrange("b (p j) d -> p b (j d)", j=TILES)
    ctx = ExitStack()
    with ctx:
        def sb(name, shape, dt=F32):
            return ctx.enter_context(nc.sbuf_tensor(name, shape, dt))

        def bank(name, n=1):
            return ctx.enter_context(nc.psum_tensor(name, [P, n * BANK], F32))

        def sem(name):
            return ctx.enter_context(nc.semaphore(name))

        ident = sb("ident", [P, P])
        ident_r = sb("ident_r", [P, P], F32R)
        ones = sb("ones", [P, P])
        ones_bf = sb("ones_bf", [P, P], BF16)
        power = sb("power", [P, PT])
        w_raw = sb("w_raw", [P, 4 * E])
        w_qkv = sb("w_qkv", [P, 4 * E])
        wo_c = sb("wo_c", [P, E])
        turned = sb("turned", [P, 2 * P])
        vec = sb("vec", [P, ROWS])
        bias_y = sb("bias_y", [P, E])
        ffn_raw = sb("ffn_raw", [P, E + RANK])
        down_raw = sb("down_raw", [PROJ + RANK, E])
        w_z = sb("w_z", [P, ZW])
        wu_raw = sb("wu_raw", [P, PT, 2, 16])
        wu_c = sb("wu_c", [P, P])
        wu_up = sb("wu_up", [P, PT, E], F32R)
        wu_low = sb("wu_low", [P, PT, E], F32R)
        sim_raw = sb("sim_raw", [PROJ, EXPERTS])
        sim_sq = sb("sim_sq", [PROJ, EXPERTS])
        sim_n = sb("sim_n", [PROJ, EXPERTS])
        sim_r = sb("sim_r", [PROJ, RANK])
        heat = sb("heat", [PROJ, 2])
        bp_t = sb("bp_t", [PROJ, P])
        BQ, BR = 0, 2 * E
        bias = sb("bias", [1, 2 * E + RW])
        part = sb("part", [1, 2, 2 * E + RW])
        part_bf = sb("part_bf", [1, 2, 2 * E + RW], BF16)
        bias_qk = sb("bias_qk", [P, 2 * E], BF16)
        bias_r = sb("bias_r", [P, 2, RW], BF16)
        mean_w = sb("mean_w", [P, 4])
        freq_c = sb("freq_c", [P, 4])
        pos = sb("pos", [P, TILES])
        expo = sb("expo", [P, ROT])
        inv_freq = sb("inv_freq", [P, ROT])
        angle = sb("angle", [P, 4, TILES, ROT])
        waves = sb("waves", [P, 2, TILES, ROT])
        cos_x = sb("cos_x", [P, TILES, 4, 2, ROT])
        sin_x = sb("sin_x", [P, TILES, 4, 2, ROT])
        code = sb("code", [P, RANK])
        share = sb("share", [P, RANK])

        x_all = sb("x_all", [P, B * T])
        y_all = sb("y_all", [P, B * T])
        v_all = sb("v_all", [P, B * TILES * VT])
        stats1, tmp1, ve1, rs1 = sb("stats1", [P, PT, 6]), sb("tmp1", [P, 3, PT]), sb("ve1", [P, PT]), sb("rs1", [P, PT])
        statsy, tmpy, vey, rsy = sb("statsy", [P, PT, 6]), sb("tmpy", [P, 3, PT]), sb("vey", [P, PT]), sb("rsy", [P, PT])
        stats2, tmp2, ve2, rs2 = sb("stats2", [P, PT, 6]), sb("tmp2", [P, 3, PT]), sb("ve2", [P, PT]), sb("rs2", [P, PT])
        statsz, tmpz, vez, rsz = sb("statsz", [P, PT, 6]), sb("tmpz", [P, 3, PT]), sb("vez", [P, PT]), sb("rsz", [P, PT])
        mean1, nm1, mean2, nm2 = sb("mean1", [P, PT]), sb("nm1", [P, PT]), sb("mean2", [P, PT]), sb("nm2", [P, PT])
        xn = sb("xn", [P, PT, E])
        xn_t = sb("xn_t", [P, PT, P])
        qk = sb("qk", [P, PT, 4, HD])
        turn = sb("turn", [P, TILES * 4, 2, ROT])
        qk_t = sb("qk_t", [P, 2, 2, T])
        neg_max = sb("neg_max", [P, UNITS, TILES])
        probs = sb("probs", [P, UNITS, TILES, T])
        probs_t = sb("probs_t", [P, UNITS, TILES, T])
        den = sb("den", [P, TILES])
        x2n = sb("x2n", [P, PT, E])
        x2n_t = sb("x2n_t", [P, PT, P])
        route = sb("route", [P, PT, 2 * RANK])
        proj_sq = sb("proj_sq", [P, PT, PROJ])
        norm2 = sb("norm2", [P, PT])
        inv_norm = sb("inv_norm", [P, PT])
        top = sb("top", [P, PT])
        below = sb("below", [P, PT, RANK])
        logit = sb("logit", [P, PT, RANK])
        expl = sb("expl", [P, PT, RANK])
        total = sb("total", [P, PT])
        key = sb("key", [P, PT, RANK])
        key_top = sb("key_top", [P, PT])
        picked = sb("picked", [P, PT, RANK])
        gate = sb("gate", [P, PT, RANK])
        gated = sb("gated", [P, PT, 2, 16], F32R)
        gated_t = sb("gated_t", [P, P], F32R)

        ps_s = [bank("ps_s0"), bank("ps_s1")]
        ps_p = bank("ps_p")
        ps_o = bank("ps_o")
        ps_q = bank("ps_q")
        ps_m = bank("ps_m")
        ps_z = bank("ps_z", 2)
        z_tile = ps_z[:, :].rearrange("p (k c) -> p k c", k=2)[:, :, 0:2 * ZW].rearrange("p k (t c) -> p k t c", t=2)

        x_loaded = sem("x_loaded")
        stored = sem("stored")
        vec_loaded, attn_loaded, ffn_loaded = sem("vec_loaded"), sem("attn_loaded"), sem("ffn_loaded")
        fold_mm, fold_dve, fold_link = sem("fold_mm"), sem("fold_dve"), sem("fold_link")
        pool_consts, dve_consts = sem("pool_consts"), sem("dve_consts")
        rope_link, rope_angles, rope_waves = sem("rope_link"), sem("rope_angles"), sem("rope_waves")
        inv_ready, ident_ready = sem("inv_ready"), sem("ident_ready")
        front_ready, tables_ready = sem("front_ready"), sem("tables_ready")
        bias_link = sem("bias_link")
        post_mm, post_dve, post_link = sem("post_mm"), sem("post_dve"), sem("post_link")
        heat_ready, sim_norm, post_ready = sem("heat_ready"), sem("sim_norm"), sem("post_ready")
        link1, var1, rstd1, pool1 = sem("link1"), sem("var1"), sem("rstd1"), sem("pool1")
        xn_ready = sem("xn_ready")
        xt_done, xt_out = sem("xt_done"), sem("xt_out")
        qkv_done, qkv_out = sem("qkv_done"), sem("qkv_out")
        rope_mid, rope_done = sem("rope_mid"), sem("rope_done")
        qkt_done, qkt_out = sem("qkt_done"), sem("qkt_out")
        scores_done = sem("scores_done")
        max_ready, probs_ready = sem("max_ready"), sem("probs_ready")
        pt_done, pt_out = sem("pt_done"), sem("pt_out")
        pv_done, den_ready, y_ready = sem("pv_done"), sem("den_ready"), sem("y_ready")
        linky, vary, rstdy = sem("linky"), sem("vary"), sem("rstdy")
        x2_ready = sem("x2_ready")
        link2, var2, rstd2, pool2 = sem("link2"), sem("var2"), sem("rstd2"), sem("pool2")
        x2n_ready = sem("x2n_ready")
        x2t_done, x2t_out = sem("x2t_done"), sem("x2t_out")
        r_done, r_out = sem("r_done"), sem("r_out")
        norm_ready, inv_norm_ready = sem("norm_ready"), sem("inv_norm_ready")
        logits_ready, exps_ready = sem("logits_ready"), sem("exps_ready")
        route_link, gated_ready = sem("route_link"), sem("gated_ready")
        dt_done, dt_out = sem("dt_done"), sem("dt_out")
        z_done, linkz, varz, rstdz = sem("z_done"), sem("linkz"), sem("varz"), sem("rstdz")
        out_ready = sem("out_ready")

        def on(s, lag):
            return not isinstance(s, int) or 0 <= s - lag < PAIRS

        def past(n, k):
            return not isinstance(n, int) or n >= k

        def rows(n, t=0, tiles=1):
            return bass.ds(n * (PT * E) + t * E, tiles * E)

        block = ctx.enter_context(nc.Block())

        @block.sync
        def _(sp):
            sp.dma_start(x_all[:, 0:2 * T].rearrange("p (b c) -> p b c", b=2), x_d[:, 0:2, :]).then_inc(x_loaded, 16)
            sp.dma_start(w_raw[:, :], w_attn).then_inc(attn_loaded, 16)
            with sp.Fori(1, PAIRS) as n:
                sp.wait_ge(x_loaded, n * 16)
                sp.dma_start(x_all[:, bass.ds(n * (2 * T), 2 * T)].rearrange("p (b c) -> p b c", b=2),
                             x_d[:, bass.ds(n * 2, 2), :]).then_inc(x_loaded, 16)
            with sp.Fori(0, PAIRS) as n:
                sp.wait_ge(out_ready, n + 1)
                sp.dma_start(out_d[:, bass.ds(n * 2, 2), :],
                             x_all[:, bass.ds(n * (2 * T), 2 * T)].rearrange("p (b c) -> p b c", b=2)).then_inc(stored, 16)
            sp.wait_ge(stored, 16 * PAIRS)

        @block.gpsimd
        def _(pool):
            pool.memset(ident[:, :], 0.0).then_inc(pool_consts, 1)
            pool.iota(pos[:, :], pattern=[[1, TILES]], base=0, channel_multiplier=TILES,
                      allow_small_or_imprecise_dtypes=True).then_inc(rope_link, 1)
            pool.iota(expo[:, :], pattern=[[1, ROT]], base=0, channel_multiplier=0,
                      allow_small_or_imprecise_dtypes=True).then_inc(rope_link, 1)
            pool.wait_ge(pool_consts, 1)
            pool.affine_select(out=ident[:, :], in_=ident[:, :], compare_op=ALU.not_equal, fill=1.0,
                               base=0, pattern=[[-1, P]], channel_multiplier=1).then_inc(pool_consts, 1)
            pool.wait_ge(pool_consts, 2)
            pool.tensor_copy(ident_r[:, :], ident[:, :]).then_inc(ident_ready, 1)
            pool.memset(power[:, :], -0.5).then_inc(pool_consts, 1)
            pool.memset(v_all[:, :].rearrange("p (t c) -> p t c", c=VW)[:, :, E:VW], 1.0).then_inc(pool_consts, 1)
            pool.memset(wu_raw[:, :, :, :], 0.0).then_inc(pool_consts, 1)
            pool.memset(gated[:, :, :, :].bitcast(F32), 0.0).then_inc(pool_consts, 1)
            pool.memset(wu_up[:, :, :].bitcast(F32), 0.0).then_inc(pool_consts, 1)
            pool.memset(wu_low[:, :, :].bitcast(F32), 0.0).then_inc(pool_consts, 1)

            def rope(n, b):
                pool.wait_ge(qkv_out, n * 4 + 2 * b + 2)
                g = qk[:, 2 * b:2 * b + 2, :, :].rearrange("p t g c -> p (t g) c")
                spatial = g[:, :, 2 * ROT:4 * ROT]
                swapped = spatial.rearrange("p g (h i) -> p g h i", h=2)[:, :, ::-1, :]
                pool.tensor_tensor(turn[:, :, :, :], swapped,
                                   sin_x[:, :, :, :, :].rearrange("p t g h i -> p (t g) h i"), ALU.mult).then_inc(rope_mid, 1)
                pool.wait_ge(rope_mid, n * 4 + 2 * b + 1)
                pool.tensor_tensor(spatial, spatial,
                                   cos_x[:, :, :, :, :].rearrange("p t g h i -> p (t g) (h i)"), ALU.mult).then_inc(rope_mid, 1)
                pool.wait_ge(rope_mid, n * 4 + 2 * b + 2)
                pool.tensor_tensor(spatial, spatial,
                                   turn[:, :, :, :].rearrange("p g h i -> p g (h i)"), ALU.add).then_inc(rope_done, 1)

            def norm_rows(n, mean, ve, rs, nm, var, link, done):
                pool.wait_ge(var, n + 1)
                pool.tensor_tensor(rs[:, :], ve[:, :], power[:, :], ALU.pow).then_inc(link, 1)
                pool.wait_ge(link, n + 1)
                pool.tensor_tensor(nm[:, :], mean[:, :], rs[:, :], ALU.mult).then_inc(done, 1)

            def step(s):
                if on(s, 0):
                    if past(s, 1):
                        pool.wait_ge(xn_ready, s)
                    norm_rows(s, mean1, ve1, rs1, nm1, var1, pool1, rstd1)
                if isinstance(s, int) and s == 0:
                    pool.wait_ge(rope_link, 6)
                    pool.tensor_tensor(inv_freq[:, :], freq_c[:, 3:4].to_broadcast([P, ROT]), expo[:, :], ALU.pow).then_inc(inv_ready, 1)
                if on(s, 1):
                    rope(s - 1, 1)
                if on(s, 3):
                    if past(s - 3, 1):
                        pool.wait_ge(x2n_ready, s - 3)
                    norm_rows(s - 3, mean2, ve2, rs2, nm2, var2, pool2, rstd2)
                if on(s, 4):
                    pool.wait_ge(varz, s - 3)
                    pool.tensor_tensor(rsz[:, :], vez[:, :], power[:, :], ALU.pow).then_inc(rstdz, 1)
                if on(s, 2):
                    pool.wait_ge(vary, s - 1)
                    pool.tensor_tensor(rsy[:, :], vey[:, :], power[:, :], ALU.pow).then_inc(rstdy, 1)
                if on(s, 0):
                    if isinstance(s, int) and s == 0:
                        pool.wait_ge(tables_ready, 4)
                    rope(s, 0)
                if on(s, 3):
                    pool.wait_ge(norm_ready, s - 2)
                    pool.tensor_tensor(inv_norm[:, :], norm2[:, :], power[:, :], ALU.pow).then_inc(inv_norm_ready, 1)

            pool.wait_ge(pool_consts, 3)
            step(0)
            pool.wait_ge(post_link, 3)
            pool.tensor_tensor(sim_n[:, :], sim_sq[:, :], power[0:PROJ, 0:EXPERTS], ALU.pow).then_inc(sim_norm, 1)
            for s in range(1, 4):
                step(s)
            with pool.Fori(4, PAIRS) as s:
                step(s)
            for s in range(PAIRS, STEPS):
                step(s)

        @block.scalar
        def _(act):
            act.dma_start(vec[:, :], vectors.partition_broadcast(P)).then_inc(vec_loaded, 16)
            act.dma_start(ffn_raw[:, :], w_ffn).then_inc(ffn_loaded, 16)
            act.dma_start(down_raw[:, :], w_down).then_inc(ffn_loaded, 16)
            act.dma_start(sim_raw[:, :], sim).then_inc(ffn_loaded, 16)
            act.wait_ge(vec_loaded, 16)
            act.activation(freq_c[:, 1:2], vec[:, AT_FREQ:AT_FREQ + 1], ACT.Exp, scale=-1.0).then_inc(rope_link, 1)
            def exps(n, u):
                act.wait_ge(max_ready, n * 4 + u + 1)
                if past(n, 1):
                    act.wait_ge(pt_done, n * 4 + u - 3)
                for j in range(TILES):
                    last = act.activation(probs[:, u, j, :], ps_s[u % 2][:, j * T:(j + 1) * T], ACT.Exp,
                                          bias=neg_max[:, u, j:j + 1])
                last.then_inc(probs_ready, 1)

            def qkt(n, b):
                act.wait_ge(qkt_done, n * 2 + b + 1)
                if past(n, 1):
                    act.wait_ge(scores_done, n * 4 + 2 * b - 2)
                act.activation(qk_t[:, b, :, :], ps_m[:, :].rearrange("p (a t) -> p a t", a=2), ACT.Copy).then_inc(qkt_out, 1)

            def probs_turned(n, u):
                act.wait_ge(pt_done, n * 4 + u + 1)
                if past(n, 1):
                    act.wait_ge(pv_done, n * 4 + u - 3)
                act.activation(probs_t[:, u, :, :], ps_p[:, :].rearrange("p (a t) -> p a t", a=TILES), ACT.Copy).then_inc(pt_out, 1)

            def qkv(n, t):
                act.wait_ge(qkv_done, n * 4 + t + 1)
                if past(n, 1):
                    act.wait_ge(qkt_done, n * 2 + t // 2 - 1)
                act.activation(qk[:, t, :, :].rearrange("p g c -> p (g c)"), ps_q[:, 0:2 * E], ACT.Copy)
                if isinstance(n, int) and n == 0 and t == 0:
                    act.wait_ge(pool_consts, 4)
                act.activation(v_all[:, bass.ds(n * (PT * VT) + t * VT, VT)].rearrange("p (h c) -> p h c", h=HEADS)[:, :, 0:E],
                               ps_q[:, 2 * E:4 * E].rearrange("p (h c) -> p h c", h=HEADS), ACT.Copy).then_inc(qkv_out, 1)

            def normalise(n, half, dst, rs, nm, ready):
                for t in (2 * half, 2 * half + 1):
                    last = act.activation(dst[:, t, :], x_all[:, rows(n, t)], ACT.Identity,
                                          bias=nm[:, t:t + 1], scale=rs[:, t:t + 1])
                if half:
                    last.then_inc(ready, 1)

            def step(s):
                f, a, o, c, d = s, s - 1, s - 2, s - 3, s - 4
                F_, A_, C_, D_ = on(s, 0), on(s, 1), on(s, 3), on(s, 4)
                if F_:
                    act.wait_ge(rstd1, f + 1)
                    if past(f, 1):
                        act.wait_ge(xt_done, f)
                    normalise(f, 0, xn, rs1, nm1, xn_ready)
                if D_:
                    act.wait_ge(dt_done, d + 1)
                    if past(d, 1):
                        act.wait_ge(z_done, d)
                    act.activation(gated_t[:, :], ps_m[:, 0:P], ACT.Copy).then_inc(dt_out, 1)
                if F_:
                    normalise(f, 1, xn, rs1, nm1, xn_ready)
                if on(s, 2):
                    probs_turned(o, 3)
                if A_:
                    exps(a, 0)
                if F_:
                    act.wait_ge(xt_done, f + 1)
                    if past(f, 1):
                        act.wait_ge(qkv_done, f * 4)
                    act.activation(xn_t[:, :, :].rearrange("p t c -> p (t c)"), ps_q[:, :], ACT.Copy).then_inc(xt_out, 1)
                if isinstance(s, int) and s == 0:
                    act.wait_ge(rope_angles, 1)
                    act.activation(waves[:, :, :, :], angle[:, 2:4, :, :], ACT.Sin).then_inc(rope_waves, 1)
                if C_:
                    act.wait_ge(rstd2, c + 1)
                    if past(c, 1):
                        act.wait_ge(x2t_done, c)
                    normalise(c, 0, x2n, rs2, nm2, x2n_ready)
                if A_:
                    qkt(a, 1)
                if C_:
                    normalise(c, 1, x2n, rs2, nm2, x2n_ready)
                if A_:
                    probs_turned(a, 0)
                if F_:
                    qkv(f, 0)
                if C_:
                    act.wait_ge(x2t_done, c + 1)
                    if past(c, 1):
                        act.wait_ge(r_done, c)
                    act.activation(x2n_t[:, :, :].rearrange("p t c -> p (t c)"), ps_m[:, :], ACT.Copy).then_inc(x2t_out, 1)
                if A_:
                    exps(a, 1)
                if F_:
                    qkv(f, 1)
                if C_:
                    act.wait_ge(r_done, c + 1)
                    if past(c, 1):
                        act.wait_ge(gated_ready, c)
                    act.activation(route[:, :, :].rearrange("p (k t) c -> p k t c", k=2), z_tile[:, :, :, PROJ:RW], ACT.Copy)
                    act.activation(proj_sq[:, :, :].rearrange("p (k t) c -> p k t c", k=2), z_tile[:, :, :, 0:PROJ],
                                   ACT.Square).then_inc(r_out, 1)
                if A_:
                    probs_turned(a, 1)
                    exps(a, 2)
                if F_:
                    qkv(f, 2)
                if A_:
                    exps(a, 3)
                if C_:
                    act.wait_ge(logits_ready, c + 1)
                    act.activation(expl[:, :, :], logit[:, :, :], ACT.Exp).then_inc(exps_ready, 1)
                if A_:
                    probs_turned(a, 2)
                if F_:
                    qkv(f, 3)
                    if isinstance(s, int) and s == 0:
                        act.wait_ge(post_link, 2)
                        act.activation(heat[:, 0:1], heat[:, 1:2], ACT.Exp).then_inc(heat_ready, 1)
                    qkt(f, 0)

            for s in range(4):
                step(s)
            with act.Fori(4, PAIRS) as s:
                step(s)
            for s in range(PAIRS, STEPS):
                step(s)

        @block.vector
        def _(dve):
            dve.memset(ones_bf[:, :], 1.0).then_inc(dve_consts, 1)
            dve.memset(ones[:, :], 1.0).then_inc(dve_consts, 1)
            dve.memset(bias_qk[:, :].bitcast(F32), 0.0).then_inc(dve_consts, 1)
            dve.memset(bias_r[:, :, :].rearrange("p t c -> p (t c)").bitcast(F32), 0.0).then_inc(dve_consts, 1)
            for x_, r in enumerate(RANKS):
                dve.memset(code[:, FIRST[x_]:FIRST[x_] + r], float(EXPERTS - x_)).then_inc(dve_consts, 1)
                dve.memset(share[:, FIRST[x_]:FIRST[x_] + r], 1.0 / r).then_inc(dve_consts, 1)

            links = {}

            def link(ins, chain, least=0):
                links[chain] = max(links.get(chain, 0), least) + 1
                ins.then_inc(chain, 1)
                dve.wait_ge(chain, links[chain])

            def split(at, n, outs):
                b, r1, r2 = bias[:, at:at + n], part[:, 0, at:at + n], part[:, 1, at:at + n]
                hi, mid = part_bf[:, 0, at:at + n], part_bf[:, 1, at:at + n]
                link(dve.tensor_copy(hi, b), bias_link)
                link(dve.tensor_tensor(r1, b, hi, ALU.subtract), bias_link)
                link(dve.tensor_copy(mid, r1), bias_link)
                link(dve.tensor_tensor(r2, r1, mid, ALU.subtract), bias_link)
                for row, src in ((0, hi), (32, mid), (64, r2)):
                    last = dve.tensor_copy(outs(row), src if len(outs(row).shape) == 2
                                           else src.unsqueeze(1).to_broadcast([1, 2, n]))
                return last

            def tile_stats(src, stats, half):
                for t in (2 * half, 2 * half + 1):
                    last = dve.bn_stats(stats[:, t, :], src(t))
                return last

            def variance(n, stats, tmp, ve, link_, var, rstd, mean=None):
                gap, dev, gap2 = tmp[:, 0, :], tmp[:, 1, :], tmp[:, 2, :]
                if past(n, 1):
                    dve.wait_ge(rstd, n)
                dve.wait_ge(link_, n * 3 + 1)
                dve.tensor_tensor(gap, stats[:, :, 1], stats[:, :, 4], ALU.subtract).then_inc(link_, 1)
                dve.scalar_tensor_tensor(dev, stats[:, :, 2], EPS * E, stats[:, :, 5], ALU.add, ALU.add)
                dve.wait_ge(link_, n * 3 + 2)
                if mean is not None:
                    dve.scalar_tensor_tensor(mean[:, :], gap, -0.5, stats[:, :, 4], ALU.mult, ALU.subtract)
                dve.scalar_tensor_tensor(gap2, gap, 0.25, gap, ALU.mult, ALU.mult).then_inc(link_, 1)
                dve.wait_ge(link_, n * 3 + 3)
                dve.scalar_tensor_tensor(ve[:, :], dev, 1.0 / E, gap2, ALU.mult, ALU.add).then_inc(var, 1)

            def row_max(n, u):
                dve.wait_ge(scores_done, n * 4 + u + 1)
                dve.tensor_reduce(neg_max[:, u, :], ps_s[u % 2][:, :].rearrange("p (j k) -> p j k", j=TILES),
                                  AX.X, ALU.max, negate=True).then_inc(max_ready, 1)

            def add_head(n, u):
                b, h = u // 2, u % 2
                dve.wait_ge(pv_done, n * 4 + u + 1)
                dve.reciprocal(den[:, :], ps_o[:, 0:TILES * VW].rearrange("p (j c) -> p j c", j=TILES)[:, :, E]).then_inc(den_ready, 1)
                dve.wait_ge(den_ready, n * 4 + u + 1)
                for j in range(TILES):
                    y = y_all[:, rows(n, 2 * b + j)]
                    last = dve.scalar_tensor_tensor(y, ps_o[:, j * VW:j * VW + E], den[:, j:j + 1],
                                                    bias_y[:, :] if h == 0 else y, ALU.mult, ALU.add)
                last.then_inc(y_ready, 1)

            def lengths(n):
                k = n * 11
                dve.wait_ge(r_out, n + 1)
                dve.tensor_reduce(norm2[:, :], proj_sq[:, :, :], AX.X, ALU.add).then_inc(route_link, 1)
                dve.tensor_reduce(top[:, :], route[:, :, RANK:2 * RANK], AX.X, ALU.max).then_inc(route_link, 1)
                dve.wait_ge(route_link, k + 1)
                dve.tensor_scalar(norm2[:, :], norm2[:, :], 1e-24, None, ALU.max).then_inc(norm_ready, 1)

            def keys(n):
                k = n * 11
                dve.wait_ge(route_link, k + 2)
                dve.tensor_tensor(below[:, :, :], route[:, :, RANK:2 * RANK],
                                  top[:, :].unsqueeze(2).to_broadcast([P, PT, RANK]), ALU.subtract).then_inc(route_link, 1)
                dve.wait_ge(route_link, k + 3)
                dve.scalar_tensor_tensor(key[:, :, :], below[:, :, :], 0.0,
                                         code[:, :].unsqueeze(1).to_broadcast([P, PT, RANK]), ALU.is_ge, ALU.mult).then_inc(route_link, 1)
                dve.wait_ge(route_link, k + 4)
                dve.tensor_reduce(key_top[:, :], key[:, :, :], AX.X, ALU.max).then_inc(route_link, 1)

            def logits(n):
                dve.wait_ge(inv_norm_ready, n + 1)
                dve.tensor_tensor(logit[:, :, :], below[:, :, :],
                                  inv_norm[:, :].unsqueeze(2).to_broadcast([P, PT, RANK]), ALU.mult).then_inc(logits_ready, 1)

            def gates(n):
                k = n * 11 + 5
                dve.wait_ge(route_link, k)
                dve.tensor_tensor(key[:, :, :], key[:, :, :],
                                  key_top[:, :].unsqueeze(2).to_broadcast([P, PT, RANK]), ALU.is_equal).then_inc(route_link, 1)
                dve.wait_ge(exps_ready, n + 1)
                dve.tensor_tensor(expl[:, :, :], expl[:, :, :],
                                  share[:, :].unsqueeze(1).to_broadcast([P, PT, RANK]), ALU.mult).then_inc(route_link, 1)
                dve.wait_ge(route_link, k + 2)
                dve.tensor_reduce(total[:, :], expl[:, :, :], AX.X, ALU.add).then_inc(route_link, 1)
                dve.tensor_tensor(picked[:, :, :], key[:, :, :], route[:, :, 0:RANK], ALU.mult)
                dve.wait_ge(route_link, k + 3)
                dve.reciprocal(total[:, :], total[:, :]).then_inc(route_link, 1)
                dve.wait_ge(route_link, k + 4)
                dve.tensor_tensor(gate[:, :, :], picked[:, :, :],
                                  total[:, :].unsqueeze(2).to_broadcast([P, PT, RANK]), ALU.mult).then_inc(route_link, 1)
                if past(n, 1):
                    dve.wait_ge(dt_done, n)
                dve.wait_ge(route_link, k + 5)
                dve.tensor_copy(gated[:, :, 0, 0:RANK], gate[:, :, :]).then_inc(route_link, 1)
                dve.wait_ge(route_link, k + 6)
                dve.tensor_tensor(gated[:, :, 1, 0:RANK], gate[:, :, :], gated[:, :, 0, 0:RANK].bitcast(F32),
                                  ALU.subtract).then_inc(gated_ready, 1)

            def add_norm(n, half, src, rs):
                for t in (2 * half, 2 * half + 1):
                    last = dve.scalar_tensor_tensor(x_all[:, rows(n, t)], src(t), rs[:, t:t + 1],
                                                    x_all[:, rows(n, t)], ALU.mult, ALU.add)
                return last

            def step(s):
                e, m, a, c, d = s, s - 1, s - 2, s - 3, s - 4
                E_, M_, A_, C_, D_ = on(s, 0), on(s, 1), on(s, 2), on(s, 3), on(s, 4)

                def x_c(t):
                    return x_all[:, rows(c, t)]

                def y_c(t):
                    return y_all[:, rows(c, t)]

                def z(t):
                    return z_tile[:, t // 2, t % 2, RW:ZW]

                if E_:
                    dve.wait_ge(x_loaded, e * 16 + 16)
                if A_:
                    row_max(a, 2)
                if E_:
                    tile_stats(lambda t: x_all[:, rows(e, t)], stats1, 0)
                    tile_stats(lambda t: x_all[:, rows(e, t)], stats1, 1).then_inc(link1, 1)
                    variance(e, stats1, tmp1, ve1, link1, var1, rstd1, mean1)
                if A_:
                    add_head(a, 0)
                if C_:
                    dve.wait_ge(rstdy, c + 1)
                    add_norm(c, 0, y_c, rsy).then_inc(x2_ready, 1)
                if D_:
                    lengths(d)
                elif C_:
                    dve.wait_ge(x2_ready, c * 2 + 1)
                if C_:
                    tile_stats(x_c, stats2, 0)
                if D_:
                    keys(d)
                if A_:
                    row_max(a, 3)
                if C_:
                    add_norm(c, 1, y_c, rsy).then_inc(x2_ready, 1)
                if D_:
                    logits(d)
                if A_:
                    add_head(a, 1)
                if D_:
                    gates(d)
                elif C_:
                    dve.wait_ge(x2_ready, c * 2 + 2)
                if C_:
                    tile_stats(x_c, stats2, 1).then_inc(link2, 1)
                if A_:
                    add_head(a, 2)
                if C_:
                    variance(c, stats2, tmp2, ve2, link2, var2, rstd2, mean2)
                if M_:
                    row_max(m, 0)
                if D_:
                    dve.wait_ge(z_done, d + 1)
                    tile_stats(z, statsz, 0)
                    tile_stats(z, statsz, 1).then_inc(linkz, 1)
                if M_:
                    row_max(m, 1)
                if D_:
                    variance(d, statsz, tmpz, vez, linkz, varz, rstdz)
                if A_:
                    add_head(a, 3)
                    tile_stats(lambda t: y_all[:, rows(a, t)], statsy, 0)
                    dve.wait_ge(y_ready, a * 4 + 4)
                if D_:
                    dve.wait_ge(rstdz, d + 1)
                    add_norm(d, 0, z, rsz)
                    add_norm(d, 1, z, rsz).then_inc(out_ready, 1)
                if A_:
                    tile_stats(lambda t: y_all[:, rows(a, t)], statsy, 1).then_inc(linky, 1)
                    variance(a, statsy, tmpy, vey, linky, vary, rstdy)

            step(0)
            dve.wait_ge(rope_link, 3)
            links[rope_link] = 3
            link(dve.tensor_scalar(freq_c[:, 2:3], freq_c[:, 1:2], 1.0, None, ALU.add), rope_link)
            link(dve.reciprocal(freq_c[:, 2:3], freq_c[:, 2:3]), rope_link)
            dve.tensor_scalar(expo[:, :], expo[:, :], -1.0 / ROT, None, ALU.mult)
            link(dve.tensor_scalar(freq_c[:, 3:4], freq_c[:, 2:3], BASE_SPAN, BASE_LOW, ALU.mult, ALU.add), rope_link)
            dve.wait_ge(attn_loaded, 16)
            link(dve.tensor_reduce(mean_w[:, 0:1], w_raw[:, 3 * E:4 * E], AX.X, ALU.add), fold_link)
            link(dve.tensor_scalar(mean_w[:, 0:1], mean_w[:, 0:1], 1.0 / E, None, ALU.mult), fold_link)
            dve.tensor_scalar(wo_c[:, :], w_raw[:, 3 * E:4 * E], mean_w[:, 0:1], None, ALU.subtract)
            dve.wait_ge(fold_mm, 1)
            dve.tensor_copy(turned[:, :], ps_z[:, 0:2 * P]).then_inc(fold_dve, 1)
            dve.tensor_scalar(w_qkv[:, 0:E], w_raw[:, 0:E], QK_SCALE, None, ALU.mult)
            dve.tensor_copy(w_qkv[:, E:2 * E], w_raw[:, E:2 * E])
            dve.tensor_scalar(bias[:, 0:E], vec[0:1, 0:E], QK_SCALE, None, ALU.mult)
            link(dve.tensor_copy(bias[:, E:2 * E], vec[0:1, E:2 * E]), bias_link)

            split(BQ, 2 * E, lambda r: bias_qk[r:r + 1, :])
            dve.wait_ge(fold_mm, 2)
            dve.tensor_copy(w_qkv[:, 2 * E:3 * E], ps_z[:, BANK:BANK + E])
            dve.tensor_copy(w_qkv[:, 3 * E:4 * E], ps_z[:, 0:E]).then_inc(front_ready, 1)
            dve.wait_ge(inv_ready, 1)
            for j in range(TILES):
                last = dve.tensor_scalar(angle[:, 0, j, :], inv_freq[:, :], pos[:, j:j + 1], ANGLE_STEP, ALU.mult, ALU.mult)
            link(last, rope_link, 6)
            link(dve.tensor_scalar(angle[:, 1, :, :], angle[:, 0, :, :], -math.pi, None, ALU.add), rope_link)
            lim = 3.1415925
            link(dve.tensor_scalar(angle[:, 2, :, :], angle[:, 1, :, :], lim, -lim, ALU.min, ALU.max), rope_link)
            link(dve.tensor_scalar(angle[:, 1, :, :], angle[:, 2, :, :], -1.0, None, ALU.mult), rope_link)
            link(dve.tensor_tensor(angle[:, 0, :, :], angle[:, 1, :, :], angle[:, 2, :, :], ALU.max), rope_link)
            dve.tensor_scalar(angle[:, 3, :, :], angle[:, 0, :, :], -1.0, math.pi / 2, ALU.mult, ALU.add).then_inc(rope_angles, 1)

            dve.wait_ge(rope_waves, 1)
            for h in range(2):
                dve.tensor_scalar(cos_x[:, :, :, h, :], waves[:, 1, :, :].unsqueeze(2).to_broadcast([P, TILES, 4, ROT]),
                                  -1.0, None, ALU.mult).then_inc(tables_ready, 1)
                dve.tensor_scalar(sin_x[:, :, :, h, :], waves[:, 0, :, :].unsqueeze(2).to_broadcast([P, TILES, 4, ROT]),
                                  1.0 - 2.0 * h, None, ALU.mult).then_inc(tables_ready, 1)
            link(dve.tensor_tensor(bias_y[:, :], ps_o[:, 0:E], vec[:, AT_BO:AT_BO + E], ALU.add), fold_link)
            link(dve.tensor_reduce(mean_w[:, 3:4], bias_y[:, :], AX.X, ALU.add), fold_link)
            link(dve.tensor_scalar(mean_w[:, 3:4], mean_w[:, 3:4], 1.0 / E, None, ALU.mult), fold_link)
            link(dve.tensor_scalar(bias_y[:, :], bias_y[:, :], mean_w[:, 3:4], None, ALU.subtract), fold_link)

            dve.wait_ge(ffn_loaded, 48)
            dve.wait_ge(pool_consts, 8)
            dve.wait_ge(dve_consts, 4 + 2 * EXPERTS)
            link(dve.tensor_tensor(sim_sq[:, :], sim_raw[:, :], sim_raw[:, :], ALU.mult), post_link)
            dve.tensor_copy(wu_raw[:, :, :, 0:RANK].rearrange("p t h c -> p (t h) c"),
                            ffn_raw[:, E:E + RANK].unsqueeze(1).to_broadcast([P, 2 * PT, RANK])).then_inc(post_dve, 1)
            link(dve.tensor_scalar(heat[:, 1:2], vec[0:PROJ, AT_TEMP:AT_TEMP + 1], CLAMP_MAX, None, ALU.min), post_link)
            dve.wait_ge(post_mm, 1)
            link(dve.tensor_scalar(sim_sq[:, :], ps_p[0:PROJ, P:P + EXPERTS], 1e-24, None, ALU.max), post_link)
            dve.wait_ge(post_mm, 2)
            link(dve.tensor_reduce(mean_w[:, 1:2], ps_z[:, 0:E], AX.X, ALU.add), post_link)
            link(dve.tensor_scalar(mean_w[:, 1:2], mean_w[:, 1:2], 1.0 / E, None, ALU.mult), post_link)
            dve.tensor_scalar(w_z[:, RW:ZW], ps_z[:, 0:E], mean_w[:, 1:2], None, ALU.subtract).then_inc(post_dve, 1)
            dve.tensor_copy(w_z[:, 0:PROJ + RANK], ps_z[:, BANK:BANK + PROJ + RANK])
            dve.tensor_copy(bp_t[:, :], ps_p[0:PROJ, 0:P]).then_inc(post_dve, 1)
            dve.wait_ge(post_mm, 3)
            link(dve.tensor_reduce(mean_w[:, 2:3], ps_z[:, 0:E], AX.X, ALU.add), post_link)
            link(dve.tensor_scalar(mean_w[:, 2:3], mean_w[:, 2:3], 1.0 / E, None, ALU.mult), post_link)
            link(dve.tensor_scalar(wu_c[:, :], ps_z[:, 0:E], mean_w[:, 2:3], None, ALU.subtract), post_link)
            for t in range(PT):
                rr = slice(32 * t, 32 * t + 32)
                last = dve.tensor_copy(wu_up[rr, t, :], wu_c[rr, :])
            link(last, post_link)
            for t in range(PT):
                rr = slice(32 * t, 32 * t + 32)
                last = dve.tensor_tensor(wu_low[rr, t, :], wu_c[rr, :], wu_up[rr, t, :].bitcast(F32), ALU.subtract)
            last.then_inc(post_dve, 1)
            dve.wait_ge(sim_norm, 1)
            dve.wait_ge(heat_ready, 1)
            link(dve.tensor_tensor(sim_n[:, :], sim_raw[:, :], sim_n[:, :], ALU.mult), post_link)
            for x_, r in enumerate(RANKS):
                last = dve.tensor_scalar(sim_r[:, FIRST[x_]:FIRST[x_] + r], sim_n[:, x_:x_ + 1].to_broadcast([PROJ, r]),
                                         heat[:, 0:1], None, ALU.mult)
            last.then_inc(post_dve, 1)
            dve.wait_ge(post_mm, 4)
            dve.tensor_copy(w_z[:, PROJ + RANK:RW], ps_z[:, BANK:BANK + RANK])
            dve.tensor_copy(bias[:, BR + PROJ + RANK:BR + RW], ps_o[0:1, 0:RANK])
            dve.tensor_copy(bias[:, BR:BR + PROJ], vec[0:1, AT_BP:AT_BP + PROJ])
            link(dve.memset(bias[:, BR + PROJ:BR + PROJ + RANK], 0.0), bias_link)
            split(BR, RW, lambda r: bias_r[r:r + 1, :, :]).then_inc(post_dve, 1)

            for s in range(1, 4):
                step(s)
            with dve.Fori(4, PAIRS) as s:
                step(s)
            for s in range(PAIRS, STEPS):
                step(s)

        @block.tensor
        def _(pe):
            def scores(n, u):
                b, h = u // 2, u % 2
                r = slice(h * HD, (h + 1) * HD)
                pe.wait_ge(qkt_out, n * 2 + b + 1)
                if past(n, 1) or u >= 2:
                    pe.wait_ge(probs_ready, n * 4 + u - 1)
                for j in range(TILES):
                    last = pe.matmul(ps_s[u % 2][:, j * T:(j + 1) * T], qk_t[r, b, 0, j * P:(j + 1) * P],
                                     qk_t[r, b, 1, :], start=True, stop=True)
                last.then_inc(scores_done, 1)

            def turn_probs(n, u):
                pe.wait_ge(probs_ready, n * 4 + u + 1)
                if past(n, 1) or u >= 1:
                    pe.wait_ge(pt_out, n * 4 + u)
                for i in range(TILES):
                    for j in range(TILES):
                        last = pe.transpose(ps_p[:, i * T + j * P:i * T + (j + 1) * P],
                                            probs[:, u, j, i * P:(i + 1) * P], ident[:, :])
                last.then_inc(pt_done, 1)

            def weigh(n, u):
                b, h = u // 2, u % 2
                pe.wait_ge(pt_out, n * 4 + u + 1)
                if past(n, 1) or u >= 1:
                    pe.wait_ge(y_ready, n * 4 + u)
                for j in range(TILES):
                    for i in range(TILES):
                        v = v_all[:, bass.ds(n * (PT * VT) + (2 * b + i) * VT + h * VW, VW)]
                        last = pe.matmul(ps_o[:, j * VW:(j + 1) * VW], probs_t[:, u, i, j * P:(j + 1) * P], v,
                                         start=(i == 0), stop=(i == TILES - 1))
                last.then_inc(pv_done, 1)

            def turn_qk(n, b):
                pe.wait_ge(rope_done, n * 2 + b + 1)
                for a in range(2):
                    for j in range(TILES):
                        last = pe.transpose(ps_m[:, a * T + j * P:a * T + (j + 1) * P],
                                            qk[:, 2 * b + j, 2 * a:2 * a + 2, :].rearrange("p g c -> p (g c)"), ident[:, :])
                last.then_inc(qkt_done, 1)

            def turn_rows(bank_, src, done):
                for t in range(PT):
                    last = pe.transpose(bank_[:, t * P:(t + 1) * P], src[:, t, :], ident[:, :])
                last.then_inc(done, 1)

            def project_qkv(n, t):
                pe.wait_ge(qkv_out if t else xt_out, n * 4 + t if t else n + 1)
                pe.matmul(ps_q[:, 0:2 * E], ones_bf[:, :], bias_qk[:, :], start=True, stop=False, skip_group_check=True)
                pe.matmul(ps_q[:, :], xn_t[:, t, :], w_qkv[:, :], start=False, stop=True, skip_group_check=True).then_inc(qkv_done, 1)

            def later_weights(part):
                if part == 0:
                    pe.wait_ge(post_link, 1)
                    pe.wait_ge(front_ready, 1)
                    pe.matmul(ps_p[0:PROJ, P:P + EXPERTS], ones[0:PROJ, 0:PROJ], sim_sq[:, :], start=True, stop=True)
                    pe.transpose(ps_p[0:PROJ, 0:P], vec[:, AT_BP:AT_BP + PROJ], ident[:, :]).then_inc(post_mm, 1)
                    pe.wait_ge(ffn_loaded, 48)
                    pe.transpose(ps_z[:, 0:E], ffn_raw[:, 0:E], ident[:, :])
                    pe.transpose(ps_z[:, BANK:BANK + PROJ + RANK], down_raw[:, :],
                                 ident[0:PROJ + RANK, 0:PROJ + RANK]).then_inc(post_mm, 1)
                elif part == 1:
                    pe.wait_ge(post_dve, 3)
                    pe.transpose(ps_z[:, 0:E], wu_raw[:, :, :, :].rearrange("p t h c -> p (t h c)"), ident[:, :]).then_inc(post_mm, 1)
                else:
                    pe.wait_ge(post_dve, 5)
                    pe.matmul(ps_z[:, BANK:BANK + RANK], down_raw[0:PROJ, :], sim_r[:, :], start=True, stop=True)
                    pe.matmul(ps_o[:, 0:RANK], bp_t[:, :], sim_r[:, :], start=True, stop=True).then_inc(post_mm, 1)

            def step(s):
                first = isinstance(s, int) and s == 0
                f, a, o, c = s, s - 1, s - 2, s - 3
                F_, A_, C_ = on(s, 0), on(s, 1), on(s, 3)
                if F_:
                    pe.wait_ge(xn_ready, f + 1)
                    if past(f, 1):
                        pe.wait_ge(qkv_out, f * 4)
                    turn_rows(ps_q, xn, xt_done)
                if on(s, 2):
                    weigh(o, 3)
                if A_:
                    pe.wait_ge(qkt_out, a * 2 + 1)
                    if past(c, 1):
                        pe.wait_ge(dt_out, c)
                    turn_qk(a, 1)
                    if isinstance(s, int) and s == 1:
                        pe.wait_ge(post_dve, 6)
                    turn_probs(a, 0)
                if first:
                    pe.wait_ge(dve_consts, 2)
                    pe.wait_ge(front_ready, 1)
                if F_:
                    project_qkv(f, 0)
                if first:
                    later_weights(0)
                if A_:
                    scores(a, 2)
                if C_:
                    pe.wait_ge(x2n_ready, c + 1)
                    if A_:
                        pe.wait_ge(qkt_out, a * 2 + 2)
                    else:
                        pe.wait_ge(dt_out, c)
                    turn_rows(ps_m, x2n, x2t_done)
                if A_:
                    weigh(a, 0)
                if F_:
                    project_qkv(f, 1)
                if C_:
                    pe.wait_ge(x2t_out, c + 1)
                    if past(c, 1):
                        pe.wait_ge(out_ready, c)
                    for k in range(2):
                        pe.matmul(z_tile[:, k, :, 0:RW], ones_bf[:, :], bias_r[:, :, :], start=True, stop=False, skip_group_check=True)
                        for t in range(2):
                            last = pe.matmul(z_tile[:, k, t, :], x2n_t[:, 2 * k + t, :], w_z[:, :], start=False, stop=False,
                                             skip_group_check=True)
                    last.then_inc(r_done, 1)
                if A_:
                    turn_probs(a, 1)
                    scores(a, 3)
                if first:
                    later_weights(1)
                if F_:
                    project_qkv(f, 2)
                if A_:
                    weigh(a, 1)
                    turn_probs(a, 2)
                if F_:
                    project_qkv(f, 3)
                if first:
                    later_weights(2)
                if F_:
                    if C_:
                        pe.wait_ge(x2t_out, c + 1)
                    elif A_:
                        pe.wait_ge(qkt_out, a * 2 + 2)
                    turn_qk(f, 0)
                if A_:
                    weigh(a, 2)
                    turn_probs(a, 3)
                if C_:
                    pe.wait_ge(gated_ready, c + 1)
                    if F_:
                        pe.wait_ge(qkt_out, f * 2 + 1)
                    else:
                        pe.wait_ge(x2t_out, c + 1)
                    pe.transpose(ps_m[:, 0:P].bitcast(F32R), gated[:, :, :, :].rearrange("p t h c -> p (t h c)"),
                                 ident_r[:, :]).then_inc(dt_done, 1)
                if F_:
                    scores(f, 0)
                if C_:
                    pe.wait_ge(dt_out, c + 1)
                    for k in range(2):
                        for wu in (wu_up, wu_low):
                            last = pe.matmul(z_tile[:, k, :, RW:ZW], gated_t[:, :], wu[:, 2 * k:2 * k + 2, :],
                                             start=False, stop=True, skip_group_check=True)
                    last.then_inc(z_done, 1)
                if F_:
                    scores(f, 1)

            pe.wait_ge(pool_consts, 2)
            pe.wait_ge(attn_loaded, 16)
            pe.transpose(ps_z[:, 0:P], w_raw[:, 2 * E:3 * E], ident[:, :])
            pe.wait_ge(vec_loaded, 16)
            pe.transpose(ps_z[:, P:2 * P], vec[:, AT_BV:AT_BV + E], ident[:, :]).then_inc(fold_mm, 1)
            pe.wait_ge(fold_dve, 1)
            pe.matmul(ps_z[:, BANK:BANK + E], turned[0:HD, 0:P], wo_c[0:HD, :], start=True, stop=True)
            pe.matmul(ps_z[:, 0:E], turned[HD:2 * HD, 0:P], wo_c[HD:2 * HD, :], start=True, stop=True)
            pe.matmul(ps_o[:, 0:E], turned[:, P:2 * P], wo_c[:, :], start=True, stop=True).then_inc(fold_mm, 1)
            for s in range(4):
                step(s)
            with pe.Fori(4, PAIRS) as s:
                step(s)
            for s in range(PAIRS, STEPS):
                step(s)


def kernel(**inputs):
    import concourse.bacc as bacc
    from concourse.bass_utils import run_bass_kernel_spmd

    def attn(n):
        return np.asarray(inputs["L0_attn_" + n])

    def ffn(n):
        return np.asarray(inputs["L0_ffn_" + n])

    arrays = {
        "x": np.ascontiguousarray(attn("x")),
        "w_attn": np.concatenate([attn("Wq"), attn("Wk"), attn("Wv"), attn("Wo")], axis=1),
        "vectors": np.concatenate([attn("bq"), attn("bk"), attn("bv"), attn("bo"), ffn("bp"), ffn("temp"), attn("nrope_freq")]),
        "w_ffn": np.concatenate([ffn("W")] + [ffn(f"Wu{i}") for i in range(EXPERTS)], axis=1),
        "w_down": np.concatenate([ffn("Wp")] + [ffn(f"Wd{i}") for i in range(EXPERTS)], axis=0),
        "sim": np.ascontiguousarray(ffn("sim")),
    }
    nc = bacc.Bacc("TRN2", target_bir_lowering=False, num_devices=1)
    args = [nc.dram_tensor(name, a.shape, mybir.dt.from_np(a.dtype), kind="ExternalInput").ap() for name, a in arrays.items()]
    out = nc.dram_tensor("out", (B, T, E), F32, kind="ExternalOutput").ap()
    layer(nc, *args, out)
    r = run_bass_kernel_spmd(nc, [arrays], core_ids=[0])
    return r.results[0]["out"]
```

```python
import math

import numpy as np

import concourse.bass as bass
from concourse import mybir
from concourse.alu_op_type import AluOpType as ALU
from contextlib import ExitStack

F32 = mybir.dt.float32
BF16 = mybir.dt.bfloat16
F32R = mybir.dt.float32r
ACT = mybir.ActivationFunctionType
AX = mybir.AxisListType

B, T, E = 16, 256, 128
P = 128
HEADS, HD = 2, 64
ROT = 16
TILES = T // P
PAIRS = B // 2
PT = 2 * TILES
UNITS = 4
VW = E + 1
VT = HEADS * VW
STEPS = PAIRS + 4
RANKS = [1, 2, 4, 8]
EXPERTS = len(RANKS)
RANK = sum(RANKS)
FIRST = [sum(RANKS[:e]) for e in range(EXPERTS)]
PROJ = 32
RW = PROJ + 2 * RANK
ZW = RW + E
BANK = 512
ROWS = 4 * E + PROJ + 2
AT_BV, AT_BO, AT_BP, AT_TEMP, AT_FREQ = 2 * E, 3 * E, 4 * E, 4 * E + PROJ, 4 * E + PROJ + 1
QK_SCALE = HD ** -0.5
EPS = 1e-5
CLAMP_MAX = float(np.log(1.0 / 0.01))
BASE_SPAN, BASE_LOW = 3400.0, 8300.0
ANGLE_STEP = 2.0 * math.pi / (T - 1)


def layer(nc, x, w_attn, vectors, w_ffn, w_down, sim, out):
    x_d = x.rearrange("b (p j) d -> p b (j d)", j=TILES)
    out_d = out.rearrange("b (p j) d -> p b (j d)", j=TILES)
    ctx = ExitStack()
    with ctx:
        def sb(name, shape, dt=F32):
            return ctx.enter_context(nc.sbuf_tensor(name, shape, dt))

        def bank(name, n=1):
            return ctx.enter_context(nc.psum_tensor(name, [P, n * BANK], F32))

        def sem(name):
            return ctx.enter_context(nc.semaphore(name))

        ident = sb("ident", [P, P])
        ident_r = sb("ident_r", [P, P], F32R)
        ones = sb("ones", [P, P])
        ones_bf = sb("ones_bf", [P, P], BF16)
        power = sb("power", [P, PT])
        eps, one = sb("eps", [P, PT]), sb("one", [P, PT])
        w_raw = sb("w_raw", [P, 4 * E])
        w_qk = sb("w_qk", [P, 2 * E])
        w_up = sb("w_up", [P, 4 * E], F32R)
        w_low = sb("w_low", [P, 4 * E], F32R)
        wo_c = sb("wo_c", [P, E])
        turned = sb("turned", [P, 2 * P])
        vec = sb("vec", [P, ROWS])
        bias_y = sb("bias_y", [P, E])
        ffn_raw = sb("ffn_raw", [P, E + RANK])
        down_raw = sb("down_raw", [PROJ + RANK, E])
        w_z = sb("w_z", [P, ZW])
        wu_raw = sb("wu_raw", [P, PT, 2, 16])
        wu_c = sb("wu_c", [P, P])
        wu_up = sb("wu_up", [P, PT, E], F32R)
        wu_low = sb("wu_low", [P, PT, E], F32R)
        sim_raw = sb("sim_raw", [PROJ, EXPERTS])
        sim_sq = sb("sim_sq", [PROJ, EXPERTS])
        sim_n = sb("sim_n", [PROJ, EXPERTS])
        sim_r = sb("sim_r", [PROJ, RANK])
        heat = sb("heat", [PROJ, 2])
        bp_t = sb("bp_t", [PROJ, P])
        bias = sb("bias", [1, RW])
        part = sb("part", [1, 2, RW])
        part_bf = sb("part_bf", [1, 2, RW], BF16)
        bias_r = sb("bias_r", [P, 2, RW], BF16)
        mean_w = sb("mean_w", [P, 5])
        freq_c = sb("freq_c", [P, 4])
        pos = sb("pos", [P, TILES])
        expo = sb("expo", [P, ROT])
        inv_freq = sb("inv_freq", [P, ROT])
        angle = sb("angle", [P, 4, TILES, ROT])
        waves = sb("waves", [P, 2, TILES, ROT])
        cos_x = sb("cos_x", [P, TILES, 4, 2, ROT])
        sin_x = sb("sin_x", [P, TILES, 4, 2, ROT])
        code = sb("code", [P, RANK])
        share = sb("share", [P, RANK])

        x_all = sb("x_all", [P, B * T])
        y_all = sb("y_all", [P, B * T])
        v_all = sb("v_all", [P, B * TILES * VT])
        stats1, tmp1, ve1, rs1 = sb("stats1", [P, PT, 6]), sb("tmp1", [P, 3, PT]), sb("ve1", [P, PT]), sb("rs1", [P, PT])
        stats2, tmp2, ve2, rs2 = sb("stats2", [P, PT, 6]), sb("tmp2", [P, 3, PT]), sb("ve2", [P, PT]), sb("rs2", [P, PT])
        sq_y, var_y, rsy = sb("sq_y", [P, PT, E]), sb("var_y", [P, PT]), sb("rsy", [P, PT])
        sq_z, var_z, rsz = sb("sq_z", [P, PT, E]), sb("var_z", [P, PT]), sb("rsz", [P, PT])
        mean1, nm1, mean2, nm2 = sb("mean1", [P, PT]), sb("nm1", [P, PT]), sb("mean2", [P, PT]), sb("nm2", [P, PT])
        xn = sb("xn", [P, PT, E])
        xn_up = sb("xn_up", [P, PT, P], F32R)
        xn_low = sb("xn_low", [P, PT, P], F32R)
        qk = sb("qk", [P, PT, 4, HD])
        turn = sb("turn", [P, 2, TILES * 4, 2, ROT])
        qk_t = sb("qk_t", [P, 2, 2, T])
        neg_max = sb("neg_max", [P, UNITS, TILES])
        probs = sb("probs", [P, UNITS, TILES, T])
        probs_t = sb("probs_t", [P, UNITS, TILES, T])
        den = sb("den", [P, TILES])
        x2n = sb("x2n", [P, PT, E])
        x2n_t = sb("x2n_t", [P, PT, P])
        route = sb("route", [P, PT, 2 * RANK])
        proj_sq = sb("proj_sq", [P, PT, PROJ])
        norm2 = sb("norm2", [P, PT])
        inv_norm = sb("inv_norm", [P, PT])
        top = sb("top", [P, PT])
        below = sb("below", [P, PT, RANK])
        logit = sb("logit", [P, PT, RANK])
        expl = sb("expl", [P, PT, RANK])
        total = sb("total", [P, PT])
        key = sb("key", [P, PT, RANK])
        key_top = sb("key_top", [P, PT])
        picked = sb("picked", [P, PT, RANK])
        gate = sb("gate", [P, PT, RANK])
        gated = sb("gated", [P, PT, 2, 16], F32R)
        gated_t = sb("gated_t", [P, P], F32R)

        ps_ss = bank("ps_ss", 2)
        ps_p = bank("ps_p")
        ps_o = bank("ps_o")
        ps_q = bank("ps_q")
        ps_m = bank("ps_m")
        ps_z = bank("ps_z", 2)
        ps_s = [ps_ss[:, 0:BANK], ps_ss[:, BANK:2 * BANK]]

        def z_tiles(n):
            two = ps_ss if last_pair(n) else ps_z
            return two[:, :].rearrange("p (k c) -> p k c", k=2)[:, :, 0:2 * ZW].rearrange("p k (t c) -> p k t c", t=2)

        def qkv_bank(n, t):
            return (ps_s[0], ps_s[1], ps_q, ps_m)[t] if isinstance(n, int) and n == 0 else ps_q

        x_loaded = sem("x_loaded")
        stored = sem("stored")
        vec_loaded, attn_loaded, ffn_loaded = sem("vec_loaded"), sem("attn_loaded"), sem("ffn_loaded")
        fold_mm, fold_dve, fold_link = sem("fold_mm"), sem("fold_dve"), sem("fold_link")
        pool_consts, dve_consts = sem("pool_consts"), sem("dve_consts")
        rope_link, rope_angles, rope_waves = sem("rope_link"), sem("rope_angles"), sem("rope_waves")
        inv_ready, ident_ready = sem("inv_ready"), sem("ident_ready")
        w_up_ready, front_ready, tables_ready = sem("w_up_ready"), sem("front_ready"), sem("tables_ready")
        bias_link = sem("bias_link")
        post_mm, post_dve, post_link = sem("post_mm"), sem("post_dve"), sem("post_link")
        heat_in, heat_ready, sim_norm = sem("heat_in"), sem("heat_ready"), sem("sim_norm")
        link1, var1, rstd1, pool1, unshifted1 = sem("link1"), sem("var1"), sem("rstd1"), sem("pool1"), sem("unshifted1")
        xn_ready = sem("xn_ready")
        xt_done, xt_out, xt_low = sem("xt_done"), sem("xt_out"), sem("xt_low")
        qkv_done, qkv_out = sem("qkv_done"), sem("qkv_out")
        rope_mid, rope_done = sem("rope_mid"), sem("rope_done")
        qkt_done, qkt_out = sem("qkt_done"), sem("qkt_out")
        scores_done = sem("scores_done")
        max_ready, probs_ready = sem("max_ready"), sem("probs_ready")
        pt_done, pt_out = sem("pt_done"), sem("pt_out")
        pv_done, den_ready, y_ready = sem("pv_done"), sem("den_ready"), sem("y_ready")
        vary, eps_y, rstdy = sem("vary"), sem("eps_y"), sem("rstdy")
        x2_ready = sem("x2_ready")
        link2, var2, rstd2, pool2 = sem("link2"), sem("var2"), sem("rstd2"), sem("pool2")
        x2n_ready = sem("x2n_ready")
        x2t_done, x2t_out = sem("x2t_done"), sem("x2t_out")
        r_done, r_out = sem("r_done"), sem("r_out")
        norm_ready, inv_norm_ready = sem("norm_ready"), sem("inv_norm_ready")
        logits_ready, exps_ready = sem("logits_ready"), sem("exps_ready")
        route_link, gated_ready = sem("route_link"), sem("gated_ready")
        dt_done, dt_out = sem("dt_done"), sem("dt_out")
        z_done, varz, eps_z, rstdz = sem("z_done"), sem("varz"), sem("eps_z"), sem("rstdz")
        out_ready = sem("out_ready")
        x2n_half, x2t_half_done, x2t_half, z_half, out_half = (
            sem("x2n_half"), sem("x2t_half_done"), sem("x2t_half"), sem("z_half"), sem("out_half"))

        def last_pair(n):
            return isinstance(n, int) and n == PAIRS - 1

        def on(s, lag):
            return not isinstance(s, int) or 0 <= s - lag < PAIRS

        def past(n, k):
            return not isinstance(n, int) or n >= k

        def rows(n, t=0, tiles=1):
            return bass.ds(n * (PT * E) + t * E, tiles * E)

        block = ctx.enter_context(nc.Block())

        @block.sync
        def _(sp):
            sp.dma_start(x_all[:, 0:2 * T].rearrange("p (b c) -> p b c", b=2), x_d[:, 0:2, :]).then_inc(x_loaded, 16)
            sp.dma_start(w_raw[:, :], w_attn).then_inc(attn_loaded, 16)
            with sp.Fori(1, PAIRS) as n:
                sp.wait_ge(x_loaded, n * 16)
                sp.dma_start(x_all[:, bass.ds(n * (2 * T), 2 * T)].rearrange("p (b c) -> p b c", b=2),
                             x_d[:, bass.ds(n * 2, 2), :]).then_inc(x_loaded, 16)
            with sp.Fori(0, PAIRS - 1) as n:
                sp.wait_ge(out_ready, n + 1)
                sp.dma_start(out_d[:, bass.ds(n * 2, 2), :],
                             x_all[:, bass.ds(n * (2 * T), 2 * T)].rearrange("p (b c) -> p b c", b=2)).then_inc(stored, 16)
            for b, ready, count in ((B - 2, out_half, 1), (B - 1, out_ready, PAIRS)):
                sp.wait_ge(ready, count)
                sp.dma_start(out_d[:, b, :], x_all[:, b * T:(b + 1) * T]).then_inc(stored, 16)
            sp.wait_ge(stored, 16 * (PAIRS + 1))

        @block.gpsimd
        def _(pool):
            pool.memset(ident[:, :], 0.0).then_inc(pool_consts, 1)
            pool.iota(pos[:, :], pattern=[[1, TILES]], base=0, channel_multiplier=TILES,
                      allow_small_or_imprecise_dtypes=True).then_inc(rope_link, 1)
            pool.iota(expo[:, :], pattern=[[1, ROT]], base=0, channel_multiplier=0,
                      allow_small_or_imprecise_dtypes=True).then_inc(rope_link, 1)
            pool.wait_ge(pool_consts, 1)
            pool.affine_select(out=ident[:, :], in_=ident[:, :], compare_op=ALU.not_equal, fill=1.0,
                               base=0, pattern=[[-1, P]], channel_multiplier=1).then_inc(pool_consts, 1)
            pool.wait_ge(pool_consts, 2)
            pool.tensor_copy(ident_r[:, :], ident[:, :]).then_inc(ident_ready, 1)
            pool.memset(one[:, :], 1.0).then_inc(pool_consts, 1)
            pool.memset(eps[:, :], EPS).then_inc(pool_consts, 1)
            pool.memset(power[:, :], -0.5).then_inc(pool_consts, 1)
            pool.memset(v_all[:, :].rearrange("p (t c) -> p t c", c=VW)[:, :, E:VW], 1.0).then_inc(pool_consts, 1)
            pool.memset(wu_raw[:, :, :, :], 0.0).then_inc(pool_consts, 1)
            pool.memset(gated[:, :, :, :].bitcast(F32), 0.0).then_inc(pool_consts, 1)
            pool.memset(wu_up[:, :, :].bitcast(F32), 0.0).then_inc(pool_consts, 1)
            pool.memset(wu_low[:, :, :].bitcast(F32), 0.0).then_inc(pool_consts, 1)

            def rope(n, b):
                pool.wait_ge(qkv_out, n * 4 + 2 * b + 2)
                g = qk[:, 2 * b:2 * b + 2, :, :].rearrange("p t g c -> p (t g) c")
                spatial = g[:, :, 2 * ROT:4 * ROT]
                swapped = spatial.rearrange("p g (h i) -> p g h i", h=2)[:, :, ::-1, :]
                pool.tensor_tensor(turn[:, b, :, :, :], swapped,
                                   sin_x[:, :, :, :, :].rearrange("p t g h i -> p (t g) h i"), ALU.mult).then_inc(rope_mid, 1)
                pool.wait_ge(rope_mid, n * 4 + 2 * b + 1)
                pool.tensor_tensor(spatial, spatial,
                                   cos_x[:, :, :, :, :].rearrange("p t g h i -> p (t g) (h i)"), ALU.mult).then_inc(rope_mid, 1)
                pool.wait_ge(rope_mid, n * 4 + 2 * b + 2)
                pool.tensor_tensor(spatial, spatial,
                                   turn[:, b, :, :, :].rearrange("p g h i -> p g (h i)"), ALU.add).then_inc(rope_done, 1)

            def norm_rows(n, mean, ve, rs, nm, var, link, done, shifted=None):
                pool.wait_ge(var, n + 1)
                pool.tensor_tensor(rs[:, :], ve[:, :], power[:, :], ALU.pow).then_inc(link, 1)
                pool.wait_ge(link, n + 1)
                last = pool.tensor_tensor(nm[:, :], mean[:, :], rs[:, :], ALU.mult)
                if shifted is not None:
                    last.then_inc(shifted, 1)
                    pool.wait_ge(shifted, n + 1)
                    last = pool.tensor_tensor(nm[:, :], nm[:, :], one[:, :], ALU.add)
                last.then_inc(done, 1)

            def inverse_lengths(n):
                pool.wait_ge(norm_ready, n + 1)
                pool.tensor_tensor(inv_norm[:, :], norm2[:, :], power[:, :], ALU.pow).then_inc(inv_norm_ready, 1)

            def factors_z(n):
                pool.wait_ge(varz, n + 1)
                pool.tensor_tensor(var_z[:, :], var_z[:, :], eps[:, :], ALU.add).then_inc(eps_z, 1)
                pool.wait_ge(eps_z, n + 1)
                if last_pair(n):
                    pool.wait_ge(out_ready, n)
                pool.tensor_tensor(rsz[:, :], var_z[:, :], power[:, :], ALU.pow).then_inc(rstdz, 1)

            def step(s):
                before_last = last_pair(s - 2)
                if on(s, 0):
                    if past(s, 1):
                        pool.wait_ge(xn_ready, s)
                    norm_rows(s, mean1, ve1, rs1, nm1, var1, pool1, rstd1, unshifted1)
                if isinstance(s, int) and s == 0:
                    pool.wait_ge(rope_link, 6)
                    pool.tensor_tensor(inv_freq[:, :], freq_c[:, 3:4].to_broadcast([P, ROT]), expo[:, :], ALU.pow).then_inc(inv_ready, 1)
                if on(s, 3):
                    pool.wait_ge(vary, s - 2)
                    pool.tensor_tensor(var_y[:, :], var_y[:, :], eps[:, :], ALU.add).then_inc(eps_y, 1)
                    pool.wait_ge(eps_y, s - 2)
                    pool.tensor_tensor(rsy[:, :], var_y[:, :], power[:, :], ALU.pow).then_inc(rstdy, 1)
                    if last_pair(s - 3):
                        inverse_lengths(s - 4)
                if on(s, 1):
                    if isinstance(s, int) and s == 1:
                        pool.wait_ge(tables_ready, 4)
                    rope(s - 1, 0)
                if on(s, 3):
                    if past(s - 3, 1):
                        pool.wait_ge(x2n_ready, s - 3)
                    norm_rows(s - 3, mean2, ve2, rs2, nm2, var2, pool2, rstd2)
                if on(s, 4) and not last_pair(s - 3):
                    factors_z(s - 4)
                if on(s, 1):
                    rope(s - 1, 1)
                if isinstance(s, int) and s == 1:
                    pool.wait_ge(post_link, 2)
                    pool.tensor_tensor(sim_n[:, :], sim_sq[:, :], power[0:PROJ, 0:EXPERTS], ALU.pow).then_inc(sim_norm, 1)
                if on(s, 3) and not before_last:
                    inverse_lengths(s - 3)
                if last_pair(s - 3):
                    factors_z(s - 4)

            pool.wait_ge(pool_consts, 5)
            for s in range(4):
                step(s)
            with pool.Fori(4, PAIRS) as s:
                step(s)
            for s in range(PAIRS, STEPS):
                step(s)

        @block.scalar
        def _(act):
            act.dma_start(vec[:, :], vectors.partition_broadcast(P)).then_inc(vec_loaded, 16)
            act.dma_start(ffn_raw[:, :], w_ffn).then_inc(ffn_loaded, 16)
            act.dma_start(down_raw[:, :], w_down).then_inc(ffn_loaded, 16)
            act.dma_start(sim_raw[:, :], sim).then_inc(ffn_loaded, 16)
            act.wait_ge(vec_loaded, 16)
            act.activation(freq_c[:, 1:2], vec[:, AT_FREQ:AT_FREQ + 1], ACT.Exp, scale=-1.0).then_inc(rope_link, 1)
            def exps(n, u):
                act.wait_ge(max_ready, n * 4 + u + 1)
                if past(n, 1):
                    act.wait_ge(pt_done, n * 4 + u - 3)
                for j in range(TILES):
                    last = act.activation(probs[:, u, j, :], ps_s[u % 2][:, j * T:(j + 1) * T], ACT.Exp,
                                          bias=neg_max[:, u, j:j + 1])
                last.then_inc(probs_ready, 1)

            def qkt(n, b):
                act.wait_ge(qkt_done, n * 2 + b + 1)
                if past(n, 1):
                    act.wait_ge(scores_done, n * 4 + 2 * b - 2)
                act.activation(qk_t[:, b, :, :], ps_m[:, :].rearrange("p (a t) -> p a t", a=2), ACT.Copy).then_inc(qkt_out, 1)

            def probs_turned(n, u):
                act.wait_ge(pt_done, n * 4 + u + 1)
                if past(n, 1):
                    act.wait_ge(pv_done, n * 4 + u - 3)
                act.activation(probs_t[:, u, :, :], ps_p[:, :].rearrange("p (a t) -> p a t", a=TILES), ACT.Copy).then_inc(pt_out, 1)

            def qkv(n, t):
                act.wait_ge(qkv_done, n * 4 + t + 1)
                if past(n, 1):
                    act.wait_ge(qkt_done, n * 2 + t // 2 - 1)
                act.activation(qk[:, t, :, :].rearrange("p g c -> p (g c)"), qkv_bank(n, t)[:, 0:2 * E], ACT.Copy)
                if isinstance(n, int) and n == 0 and t == 0:
                    act.wait_ge(pool_consts, 6)
                act.activation(v_all[:, bass.ds(n * (PT * VT) + t * VT, VT)].rearrange("p (h c) -> p h c", h=HEADS)[:, :, 0:E],
                               qkv_bank(n, t)[:, 2 * E:4 * E].rearrange("p (h c) -> p h c", h=HEADS), ACT.Copy).then_inc(qkv_out, 1)

            def normalise(n, half):
                if half == 0:
                    act.wait_ge(rstd1, n + 1)
                    if past(n, 1):
                        act.wait_ge(xt_done, n)
                for t in (2 * half, 2 * half + 1):
                    last = act.activation(xn[:, t, :], x_all[:, rows(n, t)], ACT.Identity,
                                          bias=nm1[:, t:t + 1], scale=rs1[:, t:t + 1])
                if half:
                    last.then_inc(xn_ready, 1)

            def variance(src, half, squares, var, done):
                for t in (2 * half, 2 * half + 1):
                    last = act.activation(squares[:, t, :], src(t), ACT.Square, scale=E ** -0.5, accum_out=var[:, t:t + 1])
                if half:
                    last.then_inc(done, 1)

            def variance_y(n, half):
                act.wait_ge(y_ready, n * 4 + 2 * half + 2)
                if past(n, 1) and half == 0:
                    act.wait_ge(rstdy, n)
                variance(lambda t: y_all[:, rows(n, t)], half, sq_y, var_y, vary)

            def variance_z(n, half):
                if half or not last_pair(n):
                    act.wait_ge(z_done, n + 1)
                else:
                    act.wait_ge(z_half, 1)
                if half == 0:
                    if past(n, 1):
                        act.wait_ge(rstdz, n)
                variance(lambda t: z_tiles(n)[:, t // 2, t % 2, RW:ZW], half, sq_z, var_z, varz)

            def rows_turned(src, dst, done):
                act.activation(dst[:, :, :].rearrange("p t c -> p (t c)"), src[:, :], ACT.Copy).then_inc(done, 1)

            def gated_out(n):
                act.wait_ge(dt_done, n + 1)
                if past(n, 1):
                    act.wait_ge(z_done, n)
                act.activation(gated_t[:, :], ps_m[:, 0:P], ACT.Copy).then_inc(dt_out, 1)

            def step(s):
                first = isinstance(s, int) and s == 0
                e, f, a, c, d = s, s - 1, s - 2, s - 3, s - 4
                E_, F_, A_, C_, D_ = on(s, 0), on(s, 1), on(s, 2), on(s, 3), on(s, 4)
                second = isinstance(s, int) and s == 1
                if E_ and not second:
                    normalise(e, 0)
                if F_:
                    qkv(f, 2)
                if D_ and not last_pair(c):
                    variance_z(d, 0)
                    variance_z(d, 1)
                if A_:
                    probs_turned(a, 1)
                    exps(a, 2)
                if second:
                    normalise(e, 0)
                if E_:
                    normalise(e, 1)
                if F_:
                    qkv(f, 3)
                if A_:
                    probs_turned(a, 2)
                    exps(a, 3)
                if C_ and last_pair(c):
                    act.wait_ge(x2t_half_done, 1)
                    act.wait_ge(r_done, c)
                    act.activation(x2n_t[:, 0:2, :].rearrange("p t c -> p (t c)"), ps_q[:, 0:2 * P], ACT.Copy).then_inc(x2t_half, 1)
                    act.wait_ge(x2t_done, c + 1)
                    act.activation(x2n_t[:, 2:4, :].rearrange("p t c -> p (t c)"), ps_m[:, 0:2 * P], ACT.Copy).then_inc(x2t_out, 1)
                elif C_:
                    act.wait_ge(x2t_done, c + 1)
                    if past(c, 1):
                        act.wait_ge(r_done, c)
                    rows_turned(ps_m, x2n_t, x2t_out)
                if A_:
                    variance_y(a, 0)
                if F_ and second:
                    qkt(f, 0)
                if E_:
                    act.wait_ge(xt_done, e + 1)
                    if past(e, 1):
                        act.wait_ge(qkv_done, e * 4)
                    rows_turned(ps_q, xn_up, xt_out)
                if first:
                    act.wait_ge(rope_angles, 1)
                    act.activation(waves[:, :, :, :], angle[:, 2:4, :, :], ACT.Sin).then_inc(rope_waves, 1)
                if A_:
                    probs_turned(a, 3)
                if A_ and last_pair(a):
                    variance_y(a, 1)
                if C_:
                    act.wait_ge(r_done, c + 1)
                    if past(c, 1):
                        act.wait_ge(gated_ready, c)
                    act.activation(route[:, :, :].rearrange("p (k t) c -> p k t c", k=2), z_tiles(c)[:, :, :, PROJ:RW], ACT.Copy)
                    act.activation(proj_sq[:, :, :].rearrange("p (k t) c -> p k t c", k=2), z_tiles(c)[:, :, :, 0:PROJ],
                                   ACT.Square).then_inc(r_out, 1)
                if F_ and not second:
                    qkt(f, 0)
                if A_ and not last_pair(a):
                    variance_y(a, 1)
                if last_pair(c):
                    gated_out(d)
                if C_:
                    act.wait_ge(logits_ready, c + 1)
                    act.activation(expl[:, :, :], logit[:, :, :], ACT.Exp).then_inc(exps_ready, 1)
                if last_pair(c):
                    variance_z(d, 0)
                    variance_z(d, 1)
                if E_:
                    qkv(e, 0)
                if first:
                    act.wait_ge(heat_in, 1)
                    act.activation(heat[:, 0:1], heat[:, 1:2], ACT.Exp).then_inc(heat_ready, 1)
                if F_:
                    exps(f, 0)
                    qkt(f, 1)
                if E_:
                    qkv(e, 1)
                if C_ and not last_pair(a):
                    gated_out(c)
                if F_:
                    probs_turned(f, 0)
                    exps(f, 1)

            for s in range(4):
                step(s)
            with act.Fori(4, PAIRS) as s:
                step(s)
            for s in range(PAIRS, STEPS):
                step(s)

        @block.vector
        def _(dve):
            dve.memset(ones_bf[:, :], 1.0).then_inc(dve_consts, 1)
            dve.memset(ones[:, :], 1.0).then_inc(dve_consts, 1)
            dve.memset(bias_r[:, :, :].rearrange("p t c -> p (t c)").bitcast(F32), 0.0).then_inc(dve_consts, 1)
            for x_, r in enumerate(RANKS):
                dve.memset(code[:, FIRST[x_]:FIRST[x_] + r], float(EXPERTS - x_)).then_inc(dve_consts, 1)
                dve.memset(share[:, FIRST[x_]:FIRST[x_] + r], 1.0 / r).then_inc(dve_consts, 1)

            links = {}

            def link(ins, chain, least=0):
                links[chain] = max(links.get(chain, 0), least) + 1
                ins.then_inc(chain, 1)
                dve.wait_ge(chain, links[chain])

            def split(at, n, outs):
                b, r1, r2 = bias[:, at:at + n], part[:, 0, at:at + n], part[:, 1, at:at + n]
                hi, mid = part_bf[:, 0, at:at + n], part_bf[:, 1, at:at + n]
                link(dve.tensor_copy(hi, b), bias_link)
                link(dve.tensor_tensor(r1, b, hi, ALU.subtract), bias_link)
                link(dve.tensor_copy(mid, r1), bias_link)
                link(dve.tensor_tensor(r2, r1, mid, ALU.subtract), bias_link)
                for row, src in ((0, hi), (32, mid), (64, r2)):
                    last = dve.tensor_copy(outs(row), src if len(outs(row).shape) == 2
                                           else src.unsqueeze(1).to_broadcast([1, 2, n]))
                return last

            def tile_stats(src, stats, half):
                for t in (2 * half, 2 * half + 1):
                    last = dve.bn_stats(stats[:, t, :], src(t))
                return last

            def variance(n, stats, tmp, ve, link_, var, rstd, mean=None):
                gap, dev, gap2 = tmp[:, 0, :], tmp[:, 1, :], tmp[:, 2, :]
                if past(n, 1):
                    dve.wait_ge(rstd, n)
                dve.wait_ge(link_, n * 3 + 1)
                dve.tensor_tensor(gap, stats[:, :, 1], stats[:, :, 4], ALU.subtract).then_inc(link_, 1)
                dve.scalar_tensor_tensor(dev, stats[:, :, 2], EPS * E, stats[:, :, 5], ALU.add, ALU.add)
                dve.wait_ge(link_, n * 3 + 2)
                if mean is not None:
                    dve.scalar_tensor_tensor(mean[:, :], gap, -0.5, stats[:, :, 4], ALU.mult, ALU.subtract)
                dve.scalar_tensor_tensor(gap2, gap, 0.25, gap, ALU.mult, ALU.mult).then_inc(link_, 1)
                dve.wait_ge(link_, n * 3 + 3)
                dve.scalar_tensor_tensor(ve[:, :], dev, 1.0 / E, gap2, ALU.mult, ALU.add).then_inc(var, 1)

            def normalise(n):
                dve.wait_ge(rstd2, n + 1)
                if past(n, 1):
                    dve.wait_ge(x2t_done, n)
                for t in range(PT):
                    last = dve.tensor_scalar(x2n[:, t, :], x_all[:, rows(n, t)], rs2[:, t:t + 1], nm2[:, t:t + 1],
                                             ALU.mult, ALU.add)
                    if t == 1 and last_pair(n):
                        last.then_inc(x2n_half, 1)
                last.then_inc(x2n_ready, 1)

            def low_rows(n):
                dve.wait_ge(xt_out, n + 1)
                dve.tensor_tensor(xn_low[:, :, :].rearrange("p t c -> p (t c)"), ps_q[:, :],
                                  xn_up[:, :, :].rearrange("p t c -> p (t c)").bitcast(F32), ALU.subtract).then_inc(xt_low, 1)

            def row_max(n, u):
                dve.wait_ge(scores_done, n * 4 + u + 1)
                dve.tensor_reduce(neg_max[:, u, :], ps_s[u % 2][:, :].rearrange("p (j k) -> p j k", j=TILES),
                                  AX.X, ALU.max, negate=True).then_inc(max_ready, 1)

            def add_head(n, u):
                b, h = u // 2, u % 2
                dve.wait_ge(pv_done, n * 4 + u + 1)
                dve.reciprocal(den[:, :], ps_o[:, 0:TILES * VW].rearrange("p (j c) -> p j c", j=TILES)[:, :, E]).then_inc(den_ready, 1)
                dve.wait_ge(den_ready, n * 4 + u + 1)
                for j in range(TILES):
                    y = y_all[:, rows(n, 2 * b + j)]
                    last = dve.scalar_tensor_tensor(y, ps_o[:, j * VW:j * VW + E], den[:, j:j + 1],
                                                    bias_y[:, :] if h == 0 else y, ALU.mult, ALU.add)
                last.then_inc(y_ready, 1)

            def lengths(n):
                k = n * 11
                dve.wait_ge(r_out, n + 1)
                dve.tensor_reduce(norm2[:, :], proj_sq[:, :, :], AX.X, ALU.add).then_inc(route_link, 1)
                dve.tensor_reduce(top[:, :], route[:, :, RANK:2 * RANK], AX.X, ALU.max).then_inc(route_link, 1)
                dve.wait_ge(route_link, k + 1)
                dve.tensor_scalar(norm2[:, :], norm2[:, :], 1e-24, None, ALU.max).then_inc(norm_ready, 1)

            def keys(n):
                k = n * 11
                dve.wait_ge(route_link, k + 2)
                dve.tensor_tensor(below[:, :, :], route[:, :, RANK:2 * RANK],
                                  top[:, :].unsqueeze(2).to_broadcast([P, PT, RANK]), ALU.subtract).then_inc(route_link, 1)
                dve.wait_ge(route_link, k + 3)
                dve.scalar_tensor_tensor(key[:, :, :], below[:, :, :], 0.0,
                                         code[:, :].unsqueeze(1).to_broadcast([P, PT, RANK]), ALU.is_ge, ALU.mult).then_inc(route_link, 1)
                dve.wait_ge(route_link, k + 4)
                dve.tensor_reduce(key_top[:, :], key[:, :, :], AX.X, ALU.max).then_inc(route_link, 1)

            def logits(n):
                dve.wait_ge(inv_norm_ready, n + 1)
                dve.tensor_tensor(logit[:, :, :], below[:, :, :],
                                  inv_norm[:, :].unsqueeze(2).to_broadcast([P, PT, RANK]), ALU.mult).then_inc(logits_ready, 1)

            def gates(n):
                k = n * 11 + 5
                dve.wait_ge(route_link, k)
                dve.tensor_tensor(key[:, :, :], key[:, :, :],
                                  key_top[:, :].unsqueeze(2).to_broadcast([P, PT, RANK]), ALU.is_equal).then_inc(route_link, 1)
                dve.wait_ge(exps_ready, n + 1)
                dve.tensor_tensor(expl[:, :, :], expl[:, :, :],
                                  share[:, :].unsqueeze(1).to_broadcast([P, PT, RANK]), ALU.mult).then_inc(route_link, 1)
                dve.wait_ge(route_link, k + 2)
                dve.tensor_reduce(total[:, :], expl[:, :, :], AX.X, ALU.add).then_inc(route_link, 1)
                dve.tensor_tensor(picked[:, :, :], key[:, :, :], route[:, :, 0:RANK], ALU.mult)
                dve.wait_ge(route_link, k + 3)
                dve.reciprocal(total[:, :], total[:, :]).then_inc(route_link, 1)
                dve.wait_ge(route_link, k + 4)
                dve.tensor_tensor(gate[:, :, :], picked[:, :, :],
                                  total[:, :].unsqueeze(2).to_broadcast([P, PT, RANK]), ALU.mult).then_inc(route_link, 1)
                if past(n, 1):
                    dve.wait_ge(dt_done, n)
                dve.wait_ge(route_link, k + 5)
                dve.tensor_copy(gated[:, :, 0, 0:RANK], gate[:, :, :]).then_inc(route_link, 1)
                dve.wait_ge(route_link, k + 6)
                dve.tensor_tensor(gated[:, :, 1, 0:RANK], gate[:, :, :], gated[:, :, 0, 0:RANK].bitcast(F32),
                                  ALU.subtract).then_inc(gated_ready, 1)

            def add_norm(n, half, src, rs):
                for t in (2 * half, 2 * half + 1):
                    last = dve.scalar_tensor_tensor(x_all[:, rows(n, t)], src(t), rs[:, t:t + 1],
                                                    x_all[:, rows(n, t)], ALU.mult, ALU.add)
                return last

            def later_weights(part):
                if part == 0:
                    dve.wait_ge(ffn_loaded, 48)
                    dve.wait_ge(pool_consts, 10)
                    dve.wait_ge(dve_consts, 3 + 2 * EXPERTS)
                    link(dve.tensor_tensor(sim_sq[:, :], sim_raw[:, :], sim_raw[:, :], ALU.mult), post_link)
                    dve.tensor_copy(wu_raw[:, :, :, 0:RANK].rearrange("p t h c -> p (t h) c"),
                                    ffn_raw[:, E:E + RANK].unsqueeze(1).to_broadcast([P, 2 * PT, RANK])).then_inc(post_dve, 1)
                    dve.wait_ge(post_mm, 1)
                    link(dve.tensor_scalar(sim_sq[:, :], ps_p[0:PROJ, P:P + EXPERTS], 1e-24, None, ALU.max), post_link)
                    dve.wait_ge(post_mm, 2)
                    link(dve.tensor_reduce(mean_w[:, 1:2], ps_z[:, 0:E], AX.X, ALU.add), post_link)
                    link(dve.tensor_scalar(mean_w[:, 1:2], mean_w[:, 1:2], 1.0 / E, None, ALU.mult), post_link)
                    dve.tensor_scalar(w_z[:, RW:ZW], ps_z[:, 0:E], mean_w[:, 1:2], None, ALU.subtract).then_inc(post_dve, 1)
                    dve.tensor_copy(w_z[:, 0:PROJ + RANK], ps_z[:, BANK:BANK + PROJ + RANK])
                    dve.tensor_copy(bp_t[:, :], ps_p[0:PROJ, 0:P]).then_inc(post_dve, 1)
                elif part == 1:
                    dve.wait_ge(post_mm, 3)
                    link(dve.tensor_reduce(mean_w[:, 2:3], ps_z[:, 0:E], AX.X, ALU.add), post_link)
                    link(dve.tensor_scalar(mean_w[:, 2:3], mean_w[:, 2:3], 1.0 / E, None, ALU.mult), post_link)
                    link(dve.tensor_scalar(wu_c[:, :], ps_z[:, 0:E], mean_w[:, 2:3], None, ALU.subtract), post_link)
                    for t in range(PT):
                        rr = slice(32 * t, 32 * t + 32)
                        last = dve.tensor_copy(wu_up[rr, t, :], wu_c[rr, :])
                    link(last, post_link)
                    for t in range(PT):
                        rr = slice(32 * t, 32 * t + 32)
                        last = dve.tensor_tensor(wu_low[rr, t, :], wu_c[rr, :], wu_up[rr, t, :].bitcast(F32), ALU.subtract)
                    last.then_inc(post_dve, 1)
                elif part == 2:
                    dve.wait_ge(sim_norm, 1)
                    dve.wait_ge(heat_ready, 1)
                    link(dve.tensor_tensor(sim_n[:, :], sim_raw[:, :], sim_n[:, :], ALU.mult), post_link)
                    for x_, r in enumerate(RANKS):
                        last = dve.tensor_scalar(sim_r[:, FIRST[x_]:FIRST[x_] + r], sim_n[:, x_:x_ + 1].to_broadcast([PROJ, r]),
                                                 heat[:, 0:1], None, ALU.mult)
                    last.then_inc(post_dve, 1)
                elif part == 3:
                    dve.wait_ge(post_mm, 4)
                    dve.tensor_copy(w_z[:, PROJ + RANK:RW], ps_z[:, BANK:BANK + RANK])
                    dve.tensor_copy(bias[:, PROJ + RANK:RW], ps_z[0:1, 0:RANK])
                    dve.tensor_copy(bias[:, 0:PROJ], vec[0:1, AT_BP:AT_BP + PROJ])
                    link(dve.memset(bias[:, PROJ:PROJ + RANK], 0.0), bias_link)
                    split(0, RW, lambda r: bias_r[r:r + 1, :, :]).then_inc(post_dve, 1)

            def residual(n):
                dve.wait_ge(rstdz, n + 1)
                for half in range(2):
                    last = add_norm(n, half, lambda t: z_tiles(n)[:, t // 2, t % 2, RW:ZW], rsz)
                    if half:
                        last.then_inc(out_ready, 1)
                    elif last_pair(n):
                        last.then_inc(out_half, 1)

            def step(s):
                third = isinstance(s, int) and s == 2
                e, f, a, c, d = s, s - 1, s - 2, s - 3, s - 4
                E_, F_, A_, C_, D_ = on(s, 0), on(s, 1), on(s, 2), on(s, 3), on(s, 4)

                if E_:
                    if isinstance(s, int):
                        dve.wait_ge(x_loaded, (e + 1 if e < 3 else PAIRS) * 16)
                    tile_stats(lambda t: x_all[:, rows(e, t)], stats1, 0)
                    tile_stats(lambda t: x_all[:, rows(e, t)], stats1, 1).then_inc(link1, 1)
                if C_:
                    add_head(c, 2)
                if E_:
                    variance(e, stats1, tmp1, ve1, link1, var1, rstd1, mean1)
                if F_ and not (isinstance(f, int) and f == 0):
                    low_rows(f)
                if C_ and last_pair(c):
                    add_head(c, 3)
                if D_:
                    lengths(d)
                    keys(d)
                if C_ and not last_pair(c):
                    add_head(c, 3)
                if D_ and not last_pair(c):
                    logits(d)
                if A_:
                    row_max(a, 0)
                if third:
                    later_weights(1)
                if D_ and not last_pair(c):
                    gates(d)
                if A_:
                    row_max(a, 1)
                if C_:
                    dve.wait_ge(rstdy, c + 1)
                    add_norm(c, 0, lambda t: y_all[:, rows(c, t)], rsy)
                    add_norm(c, 1, lambda t: y_all[:, rows(c, t)], rsy).then_inc(x2_ready, 1)
                    if last_pair(c):
                        logits(d)
                    dve.wait_ge(x2_ready, c + 1)
                if A_:
                    row_max(a, 2)
                if third:
                    later_weights(2)
                if C_:
                    tile_stats(lambda t: x_all[:, rows(c, t)], stats2, 0)
                    tile_stats(lambda t: x_all[:, rows(c, t)], stats2, 1).then_inc(link2, 1)
                    variance(c, stats2, tmp2, ve2, link2, var2, rstd2, mean2)
                if A_:
                    add_head(a, 0)
                    row_max(a, 3)
                if C_:
                    normalise(c)
                    if last_pair(c):
                        gates(d)
                if A_:
                    add_head(a, 1)
                if third:
                    later_weights(3)
                if last_pair(d):
                    residual(d - 1)
                if D_ and not last_pair(c):
                    residual(d)

            step(0)
            dve.wait_ge(rope_link, 3)
            links[rope_link] = 3
            link(dve.tensor_scalar(freq_c[:, 2:3], freq_c[:, 1:2], 1.0, None, ALU.add), rope_link)
            link(dve.reciprocal(freq_c[:, 2:3], freq_c[:, 2:3]), rope_link)
            dve.tensor_scalar(expo[:, :], expo[:, :], -1.0 / ROT, None, ALU.mult)
            link(dve.tensor_scalar(freq_c[:, 3:4], freq_c[:, 2:3], BASE_SPAN, BASE_LOW, ALU.mult, ALU.add), rope_link)
            dve.wait_ge(attn_loaded, 16)
            link(dve.tensor_reduce(mean_w[:, 0:1], w_raw[:, 3 * E:4 * E], AX.X, ALU.add), fold_link)
            link(dve.tensor_scalar(mean_w[:, 0:1], mean_w[:, 0:1], 1.0 / E, None, ALU.mult), fold_link)
            dve.tensor_scalar(wo_c[:, :], w_raw[:, 3 * E:4 * E], mean_w[:, 0:1], None, ALU.subtract)
            dve.wait_ge(fold_mm, 1)
            link(dve.tensor_reduce(mean_w[:, 4:5], ps_z[:, 0:P], AX.X, ALU.add), fold_link)
            link(dve.tensor_scalar(mean_w[:, 4:5], mean_w[:, 4:5], 1.0 / E, None, ALU.mult), fold_link)
            dve.tensor_scalar(turned[:, 0:P], ps_z[:, 0:P], mean_w[:, 4:5], None, ALU.subtract)
            dve.tensor_copy(turned[:, P:2 * P], ps_z[:, P:2 * P]).then_inc(fold_dve, 1)
            dve.wait_ge(fold_mm, 2)
            link(dve.tensor_tensor(w_qk[:, :], vec[:, 0:2 * E], ps_p[:, 0:2 * E], ALU.subtract), fold_link)
            link(dve.scalar_tensor_tensor(w_qk[:, :], w_qk[:, :], 1.0 / E, w_raw[:, 0:2 * E], ALU.mult, ALU.add), fold_link)
            dve.tensor_scalar(w_up[:, 0:E], w_qk[:, 0:E], QK_SCALE, None, ALU.mult)
            dve.tensor_copy(w_up[:, E:2 * E], w_qk[:, E:2 * E]).then_inc(w_up_ready, 1)
            dve.wait_ge(w_up_ready, 1)
            dve.scalar_tensor_tensor(w_low[:, 0:E], w_qk[:, 0:E], QK_SCALE, w_up[:, 0:E].bitcast(F32), ALU.mult, ALU.subtract)
            dve.tensor_tensor(w_low[:, E:2 * E], w_qk[:, E:2 * E], w_up[:, E:2 * E].bitcast(F32), ALU.subtract)
            dve.wait_ge(fold_mm, 3)
            folded = ((slice(2 * E, 3 * E), ps_z[:, BANK:BANK + E]), (slice(3 * E, 4 * E), ps_z[:, 0:E]))
            for cols, src in folded:
                last = dve.tensor_copy(w_up[:, cols], src)
            last.then_inc(w_up_ready, 1)
            dve.wait_ge(w_up_ready, 2)
            for cols, src in folded:
                last = dve.tensor_tensor(w_low[:, cols], src, w_up[:, cols].bitcast(F32), ALU.subtract)
            last.then_inc(front_ready, 1)
            low_rows(0)
            dve.tensor_scalar(heat[:, 1:2], vec[0:PROJ, AT_TEMP:AT_TEMP + 1], CLAMP_MAX, None, ALU.min).then_inc(heat_in, 1)
            dve.wait_ge(inv_ready, 1)
            for j in range(TILES):
                last = dve.tensor_scalar(angle[:, 0, j, :], inv_freq[:, :], pos[:, j:j + 1], ANGLE_STEP, ALU.mult, ALU.mult)
            link(last, rope_link, 6)
            link(dve.tensor_scalar(angle[:, 1, :, :], angle[:, 0, :, :], -math.pi, None, ALU.add), rope_link)
            lim = 3.1415925
            link(dve.tensor_scalar(angle[:, 2, :, :], angle[:, 1, :, :], lim, -lim, ALU.min, ALU.max), rope_link)
            link(dve.tensor_scalar(angle[:, 1, :, :], angle[:, 2, :, :], -1.0, None, ALU.mult), rope_link)
            link(dve.tensor_tensor(angle[:, 0, :, :], angle[:, 1, :, :], angle[:, 2, :, :], ALU.max), rope_link)
            dve.tensor_scalar(angle[:, 3, :, :], angle[:, 0, :, :], -1.0, math.pi / 2, ALU.mult, ALU.add).then_inc(rope_angles, 1)

            step(1)
            dve.wait_ge(rope_waves, 1)
            for h in range(2):
                dve.tensor_scalar(cos_x[:, :, :, h, :], waves[:, 1, :, :].unsqueeze(2).to_broadcast([P, TILES, 4, ROT]),
                                  -1.0, None, ALU.mult).then_inc(tables_ready, 1)
                dve.tensor_scalar(sin_x[:, :, :, h, :], waves[:, 0, :, :].unsqueeze(2).to_broadcast([P, TILES, 4, ROT]),
                                  1.0 - 2.0 * h, None, ALU.mult).then_inc(tables_ready, 1)
            link(dve.tensor_tensor(bias_y[:, :], ps_o[:, 0:E], vec[:, AT_BO:AT_BO + E], ALU.add), fold_link)
            link(dve.tensor_reduce(mean_w[:, 3:4], bias_y[:, :], AX.X, ALU.add), fold_link)
            link(dve.tensor_scalar(mean_w[:, 3:4], mean_w[:, 3:4], 1.0 / E, None, ALU.mult), fold_link)
            link(dve.tensor_scalar(bias_y[:, :], bias_y[:, :], mean_w[:, 3:4], None, ALU.subtract), fold_link)

            later_weights(0)
            for s in range(2, 4):
                step(s)
            with dve.Fori(4, PAIRS) as s:
                step(s)
            for s in range(PAIRS, STEPS):
                step(s)

        @block.tensor
        def _(pe):
            def scores(n, u):
                b, h = u // 2, u % 2
                r = slice(h * HD, (h + 1) * HD)
                pe.wait_ge(qkt_out, n * 2 + b + 1)
                if past(n, 1) or u >= 2:
                    pe.wait_ge(probs_ready, n * 4 + u - 1)
                for j in range(TILES):
                    last = pe.matmul(ps_s[u % 2][:, j * T:(j + 1) * T], qk_t[r, b, 0, j * P:(j + 1) * P],
                                     qk_t[r, b, 1, :], start=True, stop=True)
                last.then_inc(scores_done, 1)

            def turn_probs(n, u):
                pe.wait_ge(probs_ready, n * 4 + u + 1)
                if past(n, 1) or u >= 1:
                    pe.wait_ge(pt_out, n * 4 + u)
                for i in range(TILES):
                    for j in range(TILES):
                        last = pe.transpose(ps_p[:, i * T + j * P:i * T + (j + 1) * P],
                                            probs[:, u, j, i * P:(i + 1) * P], ident[:, :])
                last.then_inc(pt_done, 1)

            def weigh(n, u):
                b, h = u // 2, u % 2
                pe.wait_ge(pt_out, n * 4 + u + 1)
                if past(n, 1) or u >= 1:
                    pe.wait_ge(y_ready, n * 4 + u)
                for j in range(TILES):
                    for i in range(TILES):
                        v = v_all[:, bass.ds(n * (PT * VT) + (2 * b + i) * VT + h * VW, VW)]
                        last = pe.matmul(ps_o[:, j * VW:(j + 1) * VW], probs_t[:, u, i, j * P:(j + 1) * P], v,
                                         start=(i == 0), stop=(i == TILES - 1))
                last.then_inc(pv_done, 1)

            def turn_qk(n, b):
                pe.wait_ge(rope_done, n * 2 + b + 1)
                for a in range(2):
                    for j in range(TILES):
                        last = pe.transpose(ps_m[:, a * T + j * P:a * T + (j + 1) * P],
                                            qk[:, 2 * b + j, 2 * a:2 * a + 2, :].rearrange("p g c -> p (g c)"), ident[:, :])
                last.then_inc(qkt_done, 1)

            def turn_rows(bank_, src, done):
                for t in range(PT):
                    last = pe.transpose(bank_[:, t * P:(t + 1) * P], src[:, t, :], ident[:, :])
                last.then_inc(done, 1)

            def project_qkv(n, t):
                if t == 0 or (isinstance(n, int) and n == 0):
                    pe.wait_ge(xt_low, n + 1)
                else:
                    pe.wait_ge(qkv_out, n * 4 + t)
                q = qkv_bank(n, t)
                pe.matmul(q[:, :], xn_low[:, t, :], w_up[:, :], start=True, stop=False)
                pe.matmul(q[:, :], xn_up[:, t, :], w_low[:, :], start=False, stop=False)
                pe.matmul(q[:, :], xn_up[:, t, :], w_up[:, :], start=False, stop=True).then_inc(qkv_done, 1)

            def later_weights(part):
                if part == 0:
                    pe.wait_ge(post_link, 1)
                    pe.wait_ge(front_ready, 1)
                    pe.matmul(ps_p[0:PROJ, P:P + EXPERTS], ones[0:PROJ, 0:PROJ], sim_sq[:, :], start=True, stop=True)
                    pe.transpose(ps_p[0:PROJ, 0:P], vec[:, AT_BP:AT_BP + PROJ], ident[:, :]).then_inc(post_mm, 1)
                    pe.wait_ge(ffn_loaded, 48)
                    pe.transpose(ps_z[:, 0:E], ffn_raw[:, 0:E], ident[:, :])
                    pe.transpose(ps_z[:, BANK:BANK + PROJ + RANK], down_raw[:, :],
                                 ident[0:PROJ + RANK, 0:PROJ + RANK]).then_inc(post_mm, 1)
                elif part == 1:
                    pe.wait_ge(post_dve, 3)
                    pe.transpose(ps_z[:, 0:E], wu_raw[:, :, :, :].rearrange("p t h c -> p (t h c)"), ident[:, :]).then_inc(post_mm, 1)
                else:
                    pe.wait_ge(post_dve, 5)
                    pe.matmul(ps_z[:, BANK:BANK + RANK], down_raw[0:PROJ, :], sim_r[:, :], start=True, stop=True)
                    pe.matmul(ps_z[:, 0:RANK], bp_t[:, :], sim_r[:, :], start=True, stop=True).then_inc(post_mm, 1)

            def turn_gated(n, bank_free):
                pe.wait_ge(gated_ready, n + 1)
                pe.wait_ge(*bank_free)
                pe.transpose(ps_m[:, 0:P].bitcast(F32R), gated[:, :, :, :].rearrange("p t h c -> p (t h c)"),
                             ident_r[:, :]).then_inc(dt_done, 1)

            def low_rank(n):
                pe.wait_ge(dt_out, n + 1)
                for k in range(2):
                    for wu in (wu_up, wu_low):
                        last = pe.matmul(z_tiles(n)[:, k, :, RW:ZW], gated_t[:, :], wu[:, 2 * k:2 * k + 2, :],
                                         start=False, stop=True, skip_group_check=True)
                    if last_pair(n) and k == 0:
                        last.then_inc(z_half, 1)
                last.then_inc(z_done, 1)

            def step(s):
                first, second = isinstance(s, int) and s == 0, isinstance(s, int) and s == 1
                f, a, o, c = s, s - 1, s - 2, s - 3
                F_, A_, O_, C_ = on(s, 0), on(s, 1), on(s, 2), on(s, 3)
                if second:
                    pe.wait_ge(qkv_out, 4)
                    turn_qk(a, 0)
                if F_:
                    pe.wait_ge(xn_ready, f + 1)
                    if past(f, 1):
                        pe.wait_ge(qkv_out, f * 4)
                    turn_rows(ps_q, xn, xt_done)
                if second:
                    later_weights(1)
                if O_:
                    weigh(o, 2)
                    turn_probs(o, 3)
                    if last_pair(o):
                        weigh(o, 3)
                if C_:
                    if isinstance(s, int) and s == 3:
                        pe.wait_ge(post_dve, 6)
                    if last_pair(c):
                        pe.wait_ge(x2t_half, 1)
                    else:
                        pe.wait_ge(x2t_out, c + 1)
                        if past(c, 1):
                            pe.wait_ge(out_ready, c)
                    for k in range(2):
                        if last_pair(c) and k:
                            pe.wait_ge(x2t_out, c + 1)
                        pe.matmul(z_tiles(c)[:, k, :, 0:RW], ones_bf[:, :], bias_r[:, :, :], start=True, stop=False, skip_group_check=True)
                        for t in range(2):
                            last = pe.matmul(z_tiles(c)[:, k, t, :], x2n_t[:, 2 * k + t, :], w_z[:, :], start=False, stop=False,
                                             skip_group_check=True)
                    last.then_inc(r_done, 1)
                if A_ and not second:
                    if C_:
                        pe.wait_ge(x2t_out, c + 1)
                    else:
                        pe.wait_ge(qkt_out, a * 2)
                    turn_qk(a, 0)
                if O_ and not last_pair(o):
                    weigh(o, 3)
                if first:
                    pe.wait_ge(front_ready, 1)
                if A_:
                    scores(a, 0)
                if F_:
                    project_qkv(f, 0)
                if A_:
                    pe.wait_ge(qkt_out, a * 2 + 1)
                    turn_qk(a, 1)
                    scores(a, 1)
                if F_:
                    project_qkv(f, 1)
                if A_:
                    if second:
                        pe.wait_ge(post_dve, 3)
                    turn_probs(a, 0)
                if last_pair(c):
                    turn_gated(c - 1, (x2t_out, c + 1))
                    low_rank(c - 1)
                if C_ and not last_pair(o):
                    turn_gated(c, (qkt_out, a * 2 + 2) if A_ else (x2t_out, c + 1))
                if A_:
                    scores(a, 2)
                if C_ and not last_pair(o):
                    low_rank(c)
                if F_:
                    project_qkv(f, 2)
                if A_:
                    weigh(a, 0)
                    turn_probs(a, 1)
                if A_:
                    scores(a, 3)
                if F_:
                    project_qkv(f, 3)
                if first:
                    later_weights(0)
                if A_:
                    weigh(a, 1)
                    turn_probs(a, 2)
                if second:
                    later_weights(2)
                if O_ and last_pair(o):
                    for half, ready, count, to, done in ((0, x2n_half, 1, ps_q, x2t_half_done), (1, x2n_ready, PAIRS, ps_m, x2t_done)):
                        pe.wait_ge(ready, count)
                        if half:
                            pe.wait_ge(x2t_out, c + 1)
                        else:
                            pe.wait_ge(qkv_out, 4 * PAIRS)
                        for t in range(2):
                            last = pe.transpose(to[:, t * P:(t + 1) * P], x2n[:, 2 * half + t, :], ident[:, :])
                        last.then_inc(done, 1)
                elif O_:
                    pe.wait_ge(x2n_ready, o + 1)
                    if C_:
                        pe.wait_ge(dt_out, c + 1)
                    elif A_:
                        pe.wait_ge(qkt_out, a * 2 + 2)
                    turn_rows(ps_m, x2n, x2t_done)

            pe.wait_ge(pool_consts, 2)
            pe.wait_ge(attn_loaded, 16)
            pe.transpose(ps_z[:, 0:P], w_raw[:, 2 * E:3 * E], ident[:, :])
            pe.wait_ge(vec_loaded, 16)
            pe.transpose(ps_z[:, P:2 * P], vec[:, AT_BV:AT_BV + E], ident[:, :]).then_inc(fold_mm, 1)
            pe.wait_ge(dve_consts, 2)
            pe.matmul(ps_p[:, 0:2 * E], ones[:, :], w_raw[:, 0:2 * E], start=True, stop=True).then_inc(fold_mm, 1)
            pe.wait_ge(fold_dve, 1)
            pe.matmul(ps_z[:, BANK:BANK + E], turned[0:HD, 0:P], wo_c[0:HD, :], start=True, stop=True)
            pe.matmul(ps_z[:, 0:E], turned[HD:2 * HD, 0:P], wo_c[HD:2 * HD, :], start=True, stop=True)
            pe.matmul(ps_o[:, 0:E], turned[:, P:2 * P], wo_c[:, :], start=True, stop=True).then_inc(fold_mm, 1)
            for s in range(4):
                step(s)
            with pe.Fori(4, PAIRS) as s:
                step(s)
            for s in range(PAIRS, STEPS):
                step(s)


def kernel(**inputs):
    import concourse.bacc as bacc
    from concourse.bass_utils import run_bass_kernel_spmd

    def attn(n):
        return np.asarray(inputs["L0_attn_" + n])

    def ffn(n):
        return np.asarray(inputs["L0_ffn_" + n])

    arrays = {
        "x": np.ascontiguousarray(attn("x")),
        "w_attn": np.concatenate([attn("Wq"), attn("Wk"), attn("Wv"), attn("Wo")], axis=1),
        "vectors": np.concatenate([attn("bq"), attn("bk"), attn("bv"), attn("bo"), ffn("bp"), ffn("temp"), attn("nrope_freq")]),
        "w_ffn": np.concatenate([ffn("W")] + [ffn(f"Wu{i}") for i in range(EXPERTS)], axis=1),
        "w_down": np.concatenate([ffn("Wp")] + [ffn(f"Wd{i}") for i in range(EXPERTS)], axis=0),
        "sim": np.ascontiguousarray(ffn("sim")),
    }
    nc = bacc.Bacc("TRN2", target_bir_lowering=False, num_devices=1)
    args = [nc.dram_tensor(name, a.shape, mybir.dt.from_np(a.dtype), kind="ExternalInput").ap() for name, a in arrays.items()]
    out = nc.dram_tensor("out", (B, T, E), F32, kind="ExternalOutput").ap()
    layer(nc, *args, out)
    r = run_bass_kernel_spmd(nc, [arrays], core_ids=[0])
    return r.results[0]["out"]
```
